# Optimizing a Trainium2 kernel written in Bass

```python
import numpy as np
import jax
import jax.numpy as jnp

def _softmax(x, axis=-1):
    return jax.nn.softmax(x, axis=axis)

def _gelu(x):
    return jax.nn.gelu(x, approximate=True)

def _silu(x):
    return jax.nn.silu(x)

def _sigmoid(x):
    return jax.nn.sigmoid(x)

def _layernorm(x, axis=-1, eps=1e-05):
    m = jnp.mean(x, axis=axis, keepdims=True)
    v = jnp.var(x, axis=axis, keepdims=True)
    return (x - m) / jnp.sqrt(v + eps)

def _scatter_add(tgt, idx, src, axis=0):
    return tgt.at[idx].add(src)

def _segment_sum(src, seg, n):
    return jax.ops.segment_sum(src, seg, n)
kernel_name = 'mk_flamingo_gated_d2_seqx_r4_6bd244'

def setup_inputs(seed: int=0):
    np.random.seed(seed)
    _w = jnp.asarray

    def _rec_inputs():
        import jax
        import jax.numpy as jnp
        _rk = jax.random.key(seed)
        x = 7.22e-05 + 1 * jax.random.normal(jax.random.fold_in(_rk, 1), (8, 512, 256), jnp.float32)
        _lenS = 512 - jax.random.randint(jax.random.fold_in(_rk, 7), (8,), 0, max(1, 512 // 4) + 1, jnp.int32)
        _lenS2 = 64 - jax.random.randint(jax.random.fold_in(_rk, 8), (8,), 0, max(1, 64 // 4) + 1, jnp.int32)
        _ctx_1024P = jax.random.normal(jax.random.fold_in(_rk, 11), (8, 16, 256), jnp.float32)
        _ctx_1024c = jax.random.dirichlet(jax.random.fold_in(_rk, 511), 0.3 * jnp.ones((16,), jnp.float32), (8, 64))
        _ctx_1024t = jnp.einsum('bsk,bkd->bsd', _ctx_1024c, _ctx_1024P)
        _ctx_1024t = _ctx_1024t * jax.lax.rsqrt(jnp.mean(jnp.square(_ctx_1024t)) + 1e-12) * 0.953939
        ctx_1024 = 4.13588e-05 + 0.999923 * (_ctx_1024t + 0.3 * jax.random.normal(jax.random.fold_in(_rk, 611), (8, 64, 256), jnp.float32))
        _g = jax.random.normal(jax.random.fold_in(_rk, 9001), (2, 2), jnp.float32)
        _g = jnp.sign(_g) * jnp.maximum(jnp.abs(_g), 1.0) + (_g == 0) * 1.0
        g_xattn = _g[0]
        g_ffn = _g[1]
        return (x, ctx_1024, g_xattn, g_ffn)
    x, ctx_1024, g_xattn, g_ffn = _rec_inputs()

    def _L0_xattn_setup():
        import jax, jax.numpy as jnp
        import numpy as np
        C = 256
        B, SQ, SKV = (4, 512, 512)
        key = jax.random.key(seed)
        ks = jax.random.split(key, 10)
        s = 1.0 / np.sqrt(C)
        return {'x': jax.random.normal(ks[0], (B, SQ, C), jnp.float32), 'content_embeddings': jax.random.normal(ks[1], (B, SKV, C), jnp.float32), 'Wq': jax.random.normal(ks[2], (C, C), jnp.float32) * s, 'bq': jnp.zeros((C,), jnp.float32), 'Wk': jax.random.normal(ks[3], (C, C), jnp.float32) * s, 'bk': jnp.zeros((C,), jnp.float32), 'Wv': jax.random.normal(ks[4], (C, C), jnp.float32) * s, 'bv': jnp.zeros((C,), jnp.float32), 'Wo': jax.random.normal(ks[5], (C, C), jnp.float32) * s, 'bo': jnp.zeros((C,), jnp.float32)}
    _L0_xattn_all = _L0_xattn_setup()
    _L0_xattn_in = {k: v for k, v in _L0_xattn_all.items() if k in ('Wq', 'bq', 'Wk', 'bk', 'Wv', 'bv', 'Wo', 'bo')}
    del _L0_xattn_all

    def _L0_ffn_setup():
        import jax, jax.numpy as jnp
        import numpy as np
        N_EXPERTS = 8
        TOP_K = 2
        key = jax.random.key(seed)
        k1, k2, k3, k4 = jax.random.split(key, 4)
        B, T, C, H, E = (2, 512, 256, 1024, N_EXPERTS)
        x = jax.random.normal(k1, (B, T, C), dtype=jnp.float32)
        router_w = jax.random.normal(k2, (E, C), dtype=jnp.float32) * 0.02
        w1 = jax.random.normal(k3, (E, C, H), dtype=jnp.float32) * (1.0 / np.sqrt(C))
        w2 = jax.random.normal(k4, (E, H, C), dtype=jnp.float32) * (1.0 / np.sqrt(H))
        return {'x': x, 'router_w': router_w, 'w1': w1, 'w2': w2}
    _L0_ffn_all = _L0_ffn_setup()
    _L0_ffn_in = {k: v for k, v in _L0_ffn_all.items() if k in ('router_w', 'w1', 'w2')}
    del _L0_ffn_all

    def _L1_xattn_setup():
        import jax, jax.numpy as jnp
        import numpy as np
        D_MODEL = 256
        N_HEADS = 16
        HEAD_DIM = D_MODEL // N_HEADS
        key = jax.random.key(seed)
        ks = jax.random.split(key, 10)
        B, S = (2, 512)
        scale_in = 1.0 / np.sqrt(D_MODEL)
        inp = {'inputs_q': jax.random.normal(ks[0], (B, S, D_MODEL), jnp.float32), 'inputs_kv': jax.random.normal(ks[1], (B, S, D_MODEL), jnp.float32), 'Wq': jax.random.normal(ks[2], (D_MODEL, N_HEADS, HEAD_DIM), jnp.float32) * scale_in, 'Wk': jax.random.normal(ks[3], (D_MODEL, N_HEADS, HEAD_DIM), jnp.float32) * scale_in, 'Wv': jax.random.normal(ks[4], (D_MODEL, N_HEADS, HEAD_DIM), jnp.float32) * scale_in, 'bq': jnp.zeros((N_HEADS, HEAD_DIM), jnp.float32), 'bk': jnp.zeros((N_HEADS, HEAD_DIM), jnp.float32), 'bv': jnp.zeros((N_HEADS, HEAD_DIM), jnp.float32), 'Wo': jax.random.normal(ks[5], (N_HEADS, HEAD_DIM, D_MODEL), jnp.float32) * scale_in, 'bo': jnp.zeros((D_MODEL,), jnp.float32)}
        return inp
    _L1_xattn_all = _L1_xattn_setup()
    _L1_xattn_in = {k: v for k, v in _L1_xattn_all.items() if k in ('Wq', 'Wk', 'Wv', 'bq', 'bk', 'bv', 'Wo', 'bo')}
    del _L1_xattn_all

    def _L1_ffn_setup():
        import jax, jax.numpy as jnp
        import numpy as np
        B, S, D, F, E, K = (2, 512, 256, 512, 8, 2)
        key = jax.random.key(seed)
        ks = jax.random.split(key, 5)
        scale = 0.02
        return {'x': jax.random.normal(ks[0], (B, S, D), dtype=jnp.float32), 'Wg': jax.random.normal(ks[1], (E, D), dtype=jnp.float32) * scale, 'W1': jax.random.normal(ks[2], (E, F, D), dtype=jnp.float32) * scale, 'W2': jax.random.normal(ks[3], (E, F, D), dtype=jnp.float32) * scale, 'W3': jax.random.normal(ks[4], (E, D, F), dtype=jnp.float32) * scale}
    _L1_ffn_all = _L1_ffn_setup()
    _L1_ffn_in = {k: v for k, v in _L1_ffn_all.items() if k in ('Wg', 'W1', 'W2', 'W3')}
    del _L1_ffn_all
    return {'x': x, 'ctx_1024': ctx_1024, 'g_xattn': g_xattn, 'g_ffn': g_ffn, 'L0_xattn_Wq': _L0_xattn_in['Wq'], 'L0_xattn_bq': _L0_xattn_in['bq'], 'L0_xattn_Wk': _L0_xattn_in['Wk'], 'L0_xattn_bk': _L0_xattn_in['bk'], 'L0_xattn_Wv': _L0_xattn_in['Wv'], 'L0_xattn_bv': _L0_xattn_in['bv'], 'L0_xattn_Wo': _L0_xattn_in['Wo'], 'L0_xattn_bo': _L0_xattn_in['bo'], 'L0_ffn_router_w': _L0_ffn_in['router_w'], 'L0_ffn_w1': _L0_ffn_in['w1'], 'L0_ffn_w2': _L0_ffn_in['w2'], 'L1_xattn_Wq': _L1_xattn_in['Wq'], 'L1_xattn_Wk': _L1_xattn_in['Wk'], 'L1_xattn_Wv': _L1_xattn_in['Wv'], 'L1_xattn_bq': _L1_xattn_in['bq'], 'L1_xattn_bk': _L1_xattn_in['bk'], 'L1_xattn_bv': _L1_xattn_in['bv'], 'L1_xattn_Wo': _L1_xattn_in['Wo'], 'L1_xattn_bo': _L1_xattn_in['bo'], 'L1_ffn_Wg': _L1_ffn_in['Wg'], 'L1_ffn_W1': _L1_ffn_in['W1'], 'L1_ffn_W2': _L1_ffn_in['W2'], 'L1_ffn_W3': _L1_ffn_in['W3']}

def reference(x, ctx_1024, g_xattn, g_ffn, L0_xattn_Wq, L0_xattn_bq, L0_xattn_Wk, L0_xattn_bk, L0_xattn_Wv, L0_xattn_bv, L0_xattn_Wo, L0_xattn_bo, L0_ffn_router_w, L0_ffn_w1, L0_ffn_w2, L1_xattn_Wq, L1_xattn_Wk, L1_xattn_Wv, L1_xattn_bq, L1_xattn_bk, L1_xattn_bv, L1_xattn_Wo, L1_xattn_bo, L1_ffn_Wg, L1_ffn_W1, L1_ffn_W2, L1_ffn_W3):
    import jax
    import jax.numpy as jnp

    def _L0_xattn_ref(x, content_embeddings, Wq, bq, Wk, bk, Wv, bv, Wo, bo):
        import jax, jax.numpy as jnp
        import numpy as np
        C = 256
        B, SQ, SKV = (4, 512, 512)
        queries = x @ Wq.T + bq
        keys = content_embeddings @ Wk.T + bk
        values = content_embeddings @ Wv.T + bv
        scale = 1.0 / jnp.sqrt(jnp.asarray(C, x.dtype))
        scores = jnp.einsum('bqc,bkc->bqk', queries, keys) * scale
        attn = jax.nn.softmax(scores, axis=-1)
        attended = jnp.einsum('bqk,bkc->bqc', attn, values)
        out = x + attended
        return out @ Wo.T + bo

    def _L0_ffn_ref(x, router_w, w1, w2):
        import jax, jax.numpy as jnp
        import numpy as np
        N_EXPERTS = 8
        TOP_K = 2
        B, T, C = x.shape
        E = N_EXPERTS
        xf = x.reshape(-1, C)
        logits = jnp.einsum('nc,ec->ne', xf, router_w)
        probs = jax.nn.softmax(logits, axis=-1)
        top_w, top_i = jax.lax.top_k(probs, TOP_K)
        top_w = top_w / jnp.sum(top_w, axis=-1, keepdims=True)
        comb = jnp.einsum('nk,nke->ne', top_w, jax.nn.one_hot(top_i, E, dtype=xf.dtype))
        h = jax.nn.gelu(jnp.einsum('nc,ech->enh', xf, w1), approximate=False)
        y = jnp.einsum('enh,ehc->enc', h, w2)
        out = jnp.einsum('ne,enc->nc', comb, y)
        return out.reshape(B, T, C)

    def _L1_xattn_ref(inputs_q, inputs_kv, Wq, Wk, Wv, bq, bk, bv, Wo, bo):
        import jax, jax.numpy as jnp
        import numpy as np
        D_MODEL = 256
        N_HEADS = 16
        HEAD_DIM = D_MODEL // N_HEADS
        q = jnp.einsum('bsd,dhf->bshf', inputs_q, Wq) + bq
        k = jnp.einsum('bsd,dhf->bshf', inputs_kv, Wk) + bk
        v = jnp.einsum('bsd,dhf->bshf', inputs_kv, Wv) + bv
        q = q / jnp.sqrt(jnp.asarray(HEAD_DIM, q.dtype))
        attn = jnp.einsum('bqhf,bkhf->bhqk', q, k)
        attn = jax.nn.softmax(attn, axis=-1)
        ctx = jnp.einsum('bhqk,bkhf->bqhf', attn, v)
        out = jnp.einsum('bqhf,hfd->bqd', ctx, Wo) + bo
        return out

    def _L1_ffn_ref(x, Wg, W1, W2, W3):
        import jax, jax.numpy as jnp
        import numpy as np
        B, S, D, F, E, K = (2, 512, 256, 512, 8, 2)
        k = K
        scores = jnp.einsum('bsd,ed->bse', x, Wg)
        topk_scores, topk_idx = jax.lax.top_k(scores, k)
        topk_probs = jax.nn.softmax(topk_scores, axis=-1)
        h1 = jnp.einsum('bsd,efd->bsef', x, W1)
        h2 = jnp.einsum('bsd,efd->bsef', x, W2)
        hidden = jax.nn.silu(h1) * h2
        expert_out = jnp.einsum('bsef,edf->bsed', hidden, W3)
        onehot = jax.nn.one_hot(topk_idx, scores.shape[-1], dtype=x.dtype)
        gating = jnp.einsum('bsk,bske->bse', topk_probs, onehot)
        return jnp.einsum('bse,bsed->bsd', gating, expert_out)
    x = x + jnp.tanh(g_xattn[0]) * _L0_xattn_ref(_layernorm(x, axis=-1), ctx_1024, L0_xattn_Wq, L0_xattn_bq, L0_xattn_Wk, L0_xattn_bk, L0_xattn_Wv, L0_xattn_bv, L0_xattn_Wo, L0_xattn_bo)
    x = x + jnp.tanh(g_ffn[0]) * _L0_ffn_ref(_layernorm(x, axis=-1), L0_ffn_router_w, L0_ffn_w1, L0_ffn_w2)
    x = x + jnp.tanh(g_xattn[1]) * _L1_xattn_ref(_layernorm(x, axis=-1), ctx_1024, L1_xattn_Wq, L1_xattn_Wk, L1_xattn_Wv, L1_xattn_bq, L1_xattn_bk, L1_xattn_bv, L1_xattn_Wo, L1_xattn_bo)
    x = x + jnp.tanh(g_ffn[1]) * _L1_ffn_ref(_layernorm(x, axis=-1), L1_ffn_Wg, L1_ffn_W1, L1_ffn_W2, L1_ffn_W3)
    return x

_drawn_inputs = setup_inputs


def setup_inputs(seed=0):
    import zlib

    import numpy as np

    out = dict(_drawn_inputs(seed))
    spreads = {'g_ffn': (-1.0, 0.6),
     'L0_xattn_bq': (0.0, 0.1),
     'L0_xattn_bk': (0.0, 0.8),
     'L0_xattn_bv': (0.0, 0.1),
     'L0_xattn_bo': (0.0, 0.1),
     'L1_xattn_bq': (0.0, 0.554),
     'L1_xattn_bk': (0.0, 0.8),
     'L1_xattn_bv': (0.0, 0.1),
     'L1_xattn_bo': (0.0, 0.1)}
    factors = {'L1_ffn_Wg': 6.792, 'L1_ffn_W1': 6.026, 'L1_ffn_W2': 5.948, 'L1_ffn_W3': 5.966}
    for name, (base, spread) in spreads.items():
        noise = np.random.default_rng([zlib.crc32(name.encode()), seed]).standard_normal(out[name].shape)
        drawn = base * np.exp(spread * noise) if base else spread * noise
        out[name] = jnp.asarray(drawn.astype(out[name].dtype))
    for name, factor in factors.items():
        out[name] = (out[name] * factor).astype(out[name].dtype)
    return out
```

```python
from contextlib import ExitStack

import concourse.bass as bass
from concourse import mybir

F32 = mybir.dt.float32
F16 = mybir.dt.float16
I32 = mybir.dt.int32
ALU = mybir.AluOpType
ACT = mybir.ActivationFunctionType
AX = mybir.AxisListType.X
ds = bass.ds

P = 128
D = 256
DC = D // P
NB = 8
SEQ = 512
TB = SEQ // P
NT = NB * TB
TOKENS = NT * P
KEYS = 64
HEADS = 16
HD = D // HEADS
HPC = HEADS // DC
PAIRS = HEADS // 2
E = 8
EPS = 1e-5
REGION = TOKENS + P
ROW = D + 2
FT = (2 * TOKENS + E * (P - 1)) // P
PADROW = 2 * TOKENS
F0 = 4096
F1 = 3072

ARENA = 4480

XS = 2.0 ** 8
WS = 2.0 ** 6
HS = 2.0 ** 4
PS = 2.0 ** 8
FAR = -3.0e38
O_BANK = (4, 2)
S_BANK = (4, 2)
STEPS0, STEPS1 = 70, 77
RSQRT_SEED = 1597463007.0


def build(nc, x, ctxT, gates, w_attn0, b_attn0, bo0, rt0, w_attn1, b_attn1, bv1, bo1, rt1, w_ffn0, w_ffn1, out):
    rows_dram = nc.dram_tensor("expert_rows", (E * REGION + P, ROW), F32, kind="Internal").ap()
    back_dram = nc.dram_tensor("token_rows", (PADROW + TOKENS + P, D), F32, kind="Internal").ap()

    with ExitStack() as stack:
        def sb(name, shape, dt=F32):
            return stack.enter_context(nc.sbuf_tensor(name, shape, dt))

        def sem(name):
            return stack.enter_context(nc.semaphore(name))

        W = sb("W", [P, E * 2 * F0], F16)
        X = sb("X", [P, NT * D])
        stage = sb("stage", [P, 2, F0 // 2])
        arena = sb("arena", [P, ARENA])
        ident = sb("ident", [P, P])
        before = sb("before", [P, P], F16)
        ones16 = sb("ones16", [P, P], F16)
        rowscale = sb("rowscale", [1, P], F16)
        onesf = sb("onesf", [1, P])
        revidx = sb("revidx", [P, TB, E])
        region0 = sb("region0", [P, E])
        steps128 = sb("steps128", [P, E, NT])
        tileno = sb("tileno", [P, FT])
        tokid = sb("tokid", [P, NT])
        pcol = sb("pcol", [P, 1])
        padrow = sb("padrow", [P, ROW])
        hmask = sb("hmask", [P, HPC])
        smask = sb("smask", [P, 2])
        xnr = sb("xnr", [P, TB, ROW])
        stats = sb("stats", [P, TB, 6])
        mean = sb("mean", [P, TB])
        rstd = sb("rstd", [P, TB])
        lt = sb("lt", [P, TB])
        ve = sb("ve", [P, TB])
        tg = sb("tg", [P, 4])
        tgs = sb("tgs", [P, 2])
        gates_sb = sb("gates_sb", [P, 4])
        logit = sb("logit", [P, TB, E])
        eq = sb("eq", [P, TB, E])
        oh = sb("oh", [P, 2, TB, E])
        sel = sb("sel", [P, TB, E], F16)
        m1 = sb("m1", [P, TB])
        m2 = sb("m2", [P, TB])
        mi = sb("mi", [P, 2, TB])
        posr = sb("posr", [P, TB, E])
        pk = sb("pk", [P, 2, TB, E])
        slot = sb("slot", [P, 2 * TB])
        sloti = sb("sloti", [P, 2 * TB], I32)
        fill = sb("fill", [P, E])
        dif = sb("dif", [P, NT])
        wgt = sb("wgt", [P, 2, NT])
        tiles = sb("tiles", [P, E])
        endA = sb("endA", [P, E])
        endB = sb("endB", [P, E])
        code = sb("code", [P, FT])
        rowbase = sb("rowbase", [P, FT], I32)
        expert = sb("expert", [P, FT], I32)
        padslot = sb("padslot", [P, E], I32)
        rth = sb("rth", [P, DC, E], F16)
        rtl = sb("rtl", [P, DC, E], F16)
        rts = sb("rts", [P, 2, DC, E])
        idc = sb("idc", [P, 2], I32)
        idt = sb("idt", [P, 2])
        m16 = sb("m16", [P, HEADS])
        r16 = sb("r16", [P, PAIRS, 2])

        class Carver:
            def __init__(self, ap, size):
                self.ap, self.at, self.size = ap, 0, size

            def take(self, shape, dt=F32, parts=P):
                n = 1
                for s in shape:
                    n *= s
                words = n if dt == F32 else (n + 1) // 2
                v = self.ap[0:parts, self.at:self.at + words]
                self.at += words
                assert self.at <= self.size, (self.at, self.size)
                if dt != F32:
                    v = v.bitcast(dt)
                if len(shape) == 2:
                    v = v.rearrange("p (a b) -> p a b", a=shape[0])
                elif len(shape) == 3:
                    v = v.rearrange("p (a b c) -> p a b c", a=shape[0], b=shape[1])
                return v

        Wf = W[:, :].bitcast(F32)
        c = Carver(Wf[:, 7 * F0:8 * F0], F0)
        gh, gl = c.take([DC, NB * KEYS], F16), c.take([DC, NB * KEYS], F16)
        vwh, vwl = c.take([NB, D], F16), c.take([NB, D], F16)
        wo0h, wo0l = c.take([DC, D], F16), c.take([DC, D], F16)
        pth, ptl = c.take([TB, P], F16), c.take([TB, P], F16)
        c = Carver(Wf[:, 5 * F0:7 * F0], 2 * F0)
        ctx0 = c.take([DC, NB * KEYS])
        wa0 = [c.take([DC, D]) for _ in range(4)]
        kt0, vt0 = c.take([DC, NB * KEYS]), c.take([DC, NB * KEYS])
        ba0 = c.take([3, DC])
        bo0s = c.take([D], F32, 1)
        c = Carver(arena, ARENA)
        xn = c.take([TB, D])
        xth, xtl = c.take([TB, DC, P], F16), c.take([TB, DC, P], F16)
        after_xt = c.at
        smw = c.take([TB, P])
        sm = smw[:, :, 0:KEYS]
        cbh, cbl = c.take([NB * KEYS], F16, 1), c.take([NB * KEYS], F16, 1)
        c = Carver(arena, ARENA)
        c.at = after_xt
        wq1h, wq1l = c.take([DC, D], F16), c.take([DC, D], F16)
        wo1h, wo1l = c.take([DC, D], F16), c.take([DC, D], F16)
        bo1h, bo1l = c.take([D], F16, 1), c.take([D], F16, 1)
        cth, ctl = c.take([DC, P], F16), c.take([DC, P], F16)
        q32 = c.take([SEQ])
        bv1s = c.take([D], F32, 1)
        c = Carver(Wf[:, E * F1:E * F0], E * (F0 - F1))
        es = c.take([HEADS * KEYS])
        eth, etl = c.take([PAIRS, P], F16), c.take([PAIRS, P], F16)
        kbh, kbl = c.take([DC, HPC * KEYS], F16), c.take([DC, HPC * KEYS], F16)
        vbh, vbl = c.take([PAIRS, 34], F16), c.take([PAIRS, 34], F16)
        kt1h, kt1l = c.take([DC, NB * KEYS], F16), c.take([DC, NB * KEYS], F16)
        v1 = c.take([NB, D])
        qh, ql = c.take([DC, SEQ], F16), c.take([DC, SEQ], F16)
        vb32 = c.take([PAIRS, 32])
        ba1 = c.take([2, DC])
        bo1s = vb32[0:1, :, :].rearrange("p a b -> p (a b)")
        ctx1 = es.rearrange("p (a b) -> p a b", a=DC)
        wk1, wv1, wq1, wo1 = (v.bitcast(F32).rearrange("p (a b) -> p a b", a=DC) for v in (
            eth.rearrange("p a b -> p (a b)"), etl.rearrange("p a b -> p (a b)"),
            qh.rearrange("p a b -> p (a b)"), ql.rearrange("p a b -> p (a b)")))
        c = Carver(Wf[:, 5 * F1:8 * F1], 3 * F1)
        back = [[c.take([TB, D]) for _ in range(2)] for _ in range(4)]
        c = Carver(arena, ARENA)
        row_in = c.take([2, ROW])
        fxh, fxl = c.take([DC, P], F16), c.take([DC, P], F16)
        g32 = c.take([1024])
        fgh, fgl = c.take([1024], F16), c.take([1024], F16)
        y32 = c.take([2, D])
        s32 = c.take([512])
        c = Carver(arena, ARENA)
        over = c.take([E, NT])
        ended, skipped = c.take([FT, E]), c.take([FT, E])
        nended, tskip = c.take([FT]), c.take([FT])

        ps = stack.enter_context(nc.psum_tensor("ps", [P, 8, 512], F32))

        names = """consts_ready tanh_ready bias_cols
            prep0_in k0v0_ready k0_copied v0_copied g0_ready g0_copied vw0_ready vw0_copied w0_split
            x_in0 x_in w0_used0 w0_used1 w1_used0 w1_used1
            norm0_ready turned0 xh0 xl0 score0_ready score0_shifted exp0_ready prob0_ready prob0_turned ph0 pl0
            attn0_ready res0_ready lg_norm0 lg_turned0 lg_xh0 lg_xl0 logits0_ready sel0_ready count0_ready slots0_ready rows0_sent
            table0_ready pads0_sent diff0_ready e20_ready
            prep1_in kv1_ready kv1_copied w1_split
            norm1_ready turned1 xh1 xl1 q1_ready q1_evac qh1 ql1 kb1_ready score1_ready score1_shifted exp1_ready exp1_turned eh1 el1
            pv1_ready ctx1_ready ctx1_turned ch1 cl1 attn1_ready res1_ready
            lg_norm1 lg_turned1 lg_xh1 lg_xl1 logits1_ready sel1_ready count1_ready slots1_ready rows1_sent
            table1_ready pads1_sent diff1_ready e21_ready
            out_ready out_sent pool_order act_turn dve_turn pe_turn pool_turn dve_order""".split()
        S = {n: sem(n) for n in names}
        w_in = [[sem(f"w{l}_in{h}") for h in range(2)] for l in range(2)]
        w_hi = [sem(f"w{l}_hi") for l in range(2)]
        w_lo = [sem(f"w{l}_lo") for l in range(2)]
        back_in = [[sem(f"back{l}_in{r}") for r in range(4)] for l in range(2)]
        back_used = [sem(f"back{l}_used") for l in range(2)]
        F = [{n: sem(f"f{l}_{n}") for n in """row_in0 row_in1 turned xh xl ids h_ready act_done g_ready g_turned gh gl
              y_ready y_out sent0 sent1 own""".split()} for l in range(2)]

        rh_rl = ((0, 0), (1, 0), (0, 1))

        def spread(ap, axis, shape):
            return ap.unsqueeze(axis).broadcast_to(shape)

        def tok(t):
            return X[:, ds(t * D, D)]

        class Done:
            def __init__(self, eng, s):
                self.eng, self.s, self.base, self.n = eng, s, 0, 0

            def add(self, ins):
                self.n += 1
                ins.then_inc(self.s, 1)

            def wait(self):
                self.eng.wait_ge(self.s, self.base + self.n)

        FW = (F0, F1)
        HALF = (F0 // 2, F1 // 2)
        KD = (8, 4)

        def whi(l, e, at, n):
            return W[:, ds(e * (2 * FW[l]) + at, n)]

        def wlo(l, e, at, n):
            return W[:, ds(e * (2 * FW[l]) + (FW[l] + at), n)]

        block = stack.enter_context(nc.Block())

        @block.sync
        def _(sp):
            for dst, src in ((ctx0, ctxT), *((wa0[i], w_attn0[i]) for i in range(4)), (ba0, b_attn0), (bo0s, bo0),
                             (rts[:, 0], rt0), (rts[:, 1], rt1), (gates_sb[:], gates)):
                sp.dma_start(dst, src).then_inc(S["prep0_in"], 16)
            sp.dma_start(X[:, 0:TB * D].rearrange("p (t d) -> p t d", t=TB),
                         x[0:TB].rearrange("t p d -> p t d")).then_inc(S["x_in0"], 16)
            sp.dma_start(X[:, TB * D:].rearrange("p (t d) -> p t d", t=NT - TB),
                         x[TB:].rearrange("t p d -> p t d")).then_inc(S["x_in"], 16)

            def load_weights(l, src):
                for h in range(2):
                    sp.dma_start(stage[:, h, 0:HALF[l]], src[:, 0, h * HALF[l]:(h + 1) * HALF[l]]).then_inc(w_in[l][h], 16)
                with sp.Fori(1, E) as e:
                    for h in range(2):
                        sp.wait_ge(w_lo[l], 2 * e + (h - 1))
                        sp.dma_start(stage[:, h, 0:HALF[l]], src[:, ds(e, 1), h * HALF[l]:(h + 1) * HALF[l]].rearrange(
                            "p a n -> p (a n)")).then_inc(w_in[l][h], 16)

            def load_rows(l):
                sp.wait_ge(S[f"table{l}_ready"], 1)
                sp.wait_ge(S[f"rows{l}_sent"], 16 + 16 * 2 * NT)
                sp.wait_ge(S[f"pads{l}_sent"], 16 * E)

                def load(t, slot):
                    at = sp.value_load(rowbase[0:1, ds(t, 1)], min_val=0, max_val=E * REGION)
                    sp.dma_start(row_in[:, slot, :], rows_dram[ds(at, P), :]).then_inc(F[l][f"row_in{slot}"], 16)
                load(0, 0)
                load(1, 1)

                def turn(t, slot):
                    sp.wait_ge(F[l]["turned"], t - 1)
                    sp.wait_ge(F[l]["ids"], t - 1)
                    load(t, slot)
                with sp.Fori(0, (FT - 2) // 2) as m:
                    for slot in range(2):
                        turn(2 * m + (2 + slot), slot)
                for t in range(FT - (FT - 2) % 2, FT):
                    turn(t, t % 2)

            def load_back(l):
                for parity, n in ((0, (FT + 1) // 2), (1, FT // 2)):
                    sp.wait_ge(F[l][f"sent{parity}"], 16 + 16 * n)
                with sp.Fori(0, NB // 4) as m:
                    for r in range(4):
                        sp.wait_ge(back_used[l], 4 * m + (r + 1))
                        for k in range(2):
                            sp.dma_start(back[r][k], back_dram[ds(m * 4 * SEQ + (k * TOKENS + r * SEQ), SEQ), :].rearrange(
                                "(t p) d -> p t d", p=P)).then_inc(back_in[l][r], 16)

            load_weights(0, w_ffn0)
            load_rows(0)
            for dst, src in ((ctx1, ctxT), *((v, w_attn1[i]) for i, v in enumerate((wk1, wv1, wq1, wo1))),
                             (ba1, b_attn1), (bv1s, bv1), (bo1s, bo1)):
                if dst is ctx1:
                    sp.wait_ge(F[0]["y_ready"], FT)
                sp.dma_start(dst, src).then_inc(S["prep1_in"], 16)
            load_back(0)
            load_weights(1, w_ffn1)
            load_rows(1)
            load_back(1)

            with sp.Fori(0, NB) as b:
                sp.wait_ge(S["out_ready"], b + 1)
                sp.dma_start(out[ds(b * TB, TB)].rearrange("t p d -> p t d"),
                             X[:, ds(b * TB * D, TB * D)].rearrange("p (t d) -> p t d", t=TB)).then_inc(S["out_sent"], 16)
            sp.wait_ge(S["out_sent"], 16 * NB)

        @block.gpsimd
        def _(pool):
            own = Done(pool, S["pool_order"])
            g = nc.gpsimd
            own.add(g.memset(ident[:], 0.0))
            own.add(g.memset(before[:], 1.0))
            own.add(g.memset(ones16[:], 1.0))
            own.add(g.memset(rowscale[:], XS))
            own.add(g.memset(onesf[:], 1.0))
            own.add(g.memset(hmask[:], 1.0))
            own.add(g.memset(smask[:], 1.0))
            own.add(g.memset(padrow[:], 0.0))
            own.add(g.iota(revidx[:], [[0, TB], [-1, E]], base=E, channel_multiplier=0, allow_small_or_imprecise_dtypes=True))
            own.add(g.iota(region0[:], [[REGION, E]], base=0, channel_multiplier=0, allow_small_or_imprecise_dtypes=True))
            own.add(g.iota(steps128[:], [[0, E], [P, NT]], base=0, channel_multiplier=0, allow_small_or_imprecise_dtypes=True))
            own.add(g.iota(tileno[:], [[1, FT]], base=0, channel_multiplier=0, allow_small_or_imprecise_dtypes=True))
            own.add(g.iota(tokid[:], [[P, NT]], base=0, channel_multiplier=1, allow_small_or_imprecise_dtypes=True))
            own.add(g.iota(pcol[:], [[0, 1]], base=0, channel_multiplier=1, allow_small_or_imprecise_dtypes=True))
            own.wait()
            own.add(g.affine_select(ident[:], ident[:], pattern=[[-1, P]], compare_op=ALU.not_equal, fill=1.0, base=0, channel_multiplier=1))
            own.add(g.affine_select(before[:], before[:], pattern=[[1, P]], compare_op=ALU.is_ge, fill=0.0, base=-1, channel_multiplier=-1))
            own.add(g.affine_select(hmask[:], hmask[:], pattern=[[-HD, HPC]], compare_op=ALU.is_ge, fill=0.0, base=0, channel_multiplier=1))
            own.add(g.affine_select(smask[:], smask[:], pattern=[[-KEYS, 2]], compare_op=ALU.is_ge, fill=0.0, base=0, channel_multiplier=1))
            own.add(g.iota(padrow[:, D:D + 1], [[0, 1]], base=PADROW, channel_multiplier=1, allow_small_or_imprecise_dtypes=True))
            own.wait()
            own.add(g.affine_select(hmask[:], hmask[:], pattern=[[HD, HPC]], compare_op=ALU.is_ge, fill=0.0, base=HD - 1, channel_multiplier=-1))
            own.add(g.affine_select(smask[:], smask[:], pattern=[[KEYS, 2]], compare_op=ALU.is_ge, fill=0.0, base=KEYS - 1, channel_multiplier=-1))
            own.wait()
            pool.sem_inc(S["consts_ready"], 1)

            def scatter(dst, index, src, done):
                g.indirect_dma_start(dst, bass.IndirectOffsetOnAxis(ap=index, axis=0), src, None).then_inc(done, 16)

            for l in range(2):
                sent = S[f"rows{l}_sent"]
                pool.dma_start(rows_dram[E * REGION:E * REGION + P, :], padrow[:]).then_inc(sent, 16)
                with pool.Fori(0, NB) as b:
                    pool.wait_ge(S[f"slots{l}_ready"], b + 1)
                    pool.sem_inc(S["pool_turn"], 1)
                    for j in range(TB):
                        for k in range(2):
                            scatter(rows_dram, sloti[:, k * TB + j:k * TB + j + 1], xnr[:, j, :], sent)
                pool.wait_ge(S[f"table{l}_ready"], 1)
                for e in range(E):
                    scatter(rows_dram, padslot[:, e:e + 1], padrow[:], S[f"pads{l}_sent"])

                for parity in range(2):
                    pool.dma_start(back_dram[PADROW + (1 + parity) * P:PADROW + (2 + parity) * P, :],
                                   padrow[:, 0:D]).then_inc(F[l][f"sent{parity}"], 16)

                def send(t, half, parity):
                    pool.wait_ge(F[l]["y_out"], t + 2)
                    pool.wait_ge(F[l]["ids"], t + 1)
                    pool.wait_ge(F[l][f"sent{1 - parity}"], 16 * half + 16 * (1 + parity))
                    pool.sem_inc(S["pool_turn"], 1)
                    scatter(back_dram, idc[:, parity:parity + 1], y32[:, parity, :], F[l][f"sent{parity}"])
                with pool.Fori(0, FT // 2) as m:
                    for parity in range(2):
                        send(2 * m + parity, m, parity)
                if FT % 2:
                    send(FT - 1, FT // 2, 0)

        @block.scalar
        def _(act):
            a = nc.scalar

            def hi(dst, src, scale, done):
                a.activation(dst, src, ACT.Copy, scale=scale).then_inc(done, 1)

            def split_weights(l, e, h):
                act.wait_ge(w_in[l][h], 16 * e + 16)
                if l == 1:
                    act.wait_ge(F[0]["y_ready"], FT)
                act.sem_inc(S["act_turn"], 1)
                hi(whi(l, e, h * HALF[l], HALF[l]), stage[:, h, 0:HALF[l]], WS, w_hi[l])

            def logits_turn(l, b):
                for h in range(2):
                    act.wait_ge(S[f"lg_turned{l}"], 2 * b + (h + 1))
                    hi(xth[:, 2 * h:2 * h + 2], ps[:, h, :], 1.0, S[f"lg_xh{l}"])

            act.wait_ge(S["prep0_in"], 160)
            a.activation(tg[:], gates_sb[:], ACT.Tanh).then_inc(S["tanh_ready"], 1)

            def attention0(b, weights):
                for h in range(2):
                    act.wait_ge(S["turned0"], 2 * b + (h + 1))
                    hi(xth[:, 2 * h:2 * h + 2], ps[:, h, :], 1.0, S["xh0"])
                if weights:
                    split_weights(0, b, 0)
                act.wait_ge(S["score0_shifted"], b + 1)
                a.activation(sm, sm, ACT.Exp, scale=1.0 / (XS * WS)).then_inc(S["exp0_ready"], 1)
                act.wait_ge(S["prob0_turned"], b + 1)
                hi(pth, ps[:, 3, :], PS, S["ph0"])
                if weights:
                    split_weights(0, b, 1)
                logits_turn(0, b)
            with act.Fori(0, NB - 1) as b:
                attention0(b, True)
            attention0(NB - 1, False)
            for h in range(2):
                split_weights(0, E - 1, h)

            def gate_weights(l):
                act.wait_ge(S[f"diff{l}_ready"], 1)
                a.activation(dif[:], dif[:], ACT.Exp, scale=1.0 / (XS * WS)).then_inc(S[f"e2{l}_ready"], 1)
            gate_weights(0)

            def experts(l):
                f = F[l]

                def xhi(t):
                    act.wait_ge(f["turned"], t + 1)
                    hi(fxh, ps[:, 0, 0:D], 1.0, f["xh"])

                def gate(t, first):
                    if l == 0:
                        for h in range(2):
                            act.wait_ge(f["h_ready"], 2 * t + (h + 1))
                            if not first:
                                act.wait_ge(f["g_turned"], 2 * t + (h - 1))
                            a.activation(g32[:, h * 512:(h + 1) * 512], ps[:, 1 + h, :], ACT.Gelu,
                                         scale=1.0 / (XS * WS)).then_inc(f["act_done"], 1)
                    else:
                        act.wait_ge(f["h_ready"], 2 * t + 1)
                        if not first:
                            act.wait_ge(f["g_ready"], t)
                        a.activation(s32, ps[:, 1, :], ACT.Silu, scale=1.0 / (XS * WS)).then_inc(f["act_done"], 1)

                def ghi(t, first):
                    for h in range(2 - l):
                        act.wait_ge(f["g_turned"], (2 - l) * t + (h + 1))
                        if not first:
                            act.wait_ge(f["y_ready"], t)
                        hi(fgh[:, h * 512:(h + 1) * 512], ps[:, 3 + h, :], HS, f["gh"])
                xhi(0)
                gate(0, True)
                xhi(1)
                ghi(0, True)
                with act.Fori(1, FT - 1) as t:
                    gate(t, False)
                    xhi(t + 1)
                    ghi(t, False)
                gate(FT - 1, False)
                ghi(FT - 1, False)
            experts(0)

            def attention1(b):
                for h in range(2):
                    act.wait_ge(S["turned1"], 2 * b + (h + 1))
                    hi(xth[:, 2 * h:2 * h + 2], ps[:, h, :], 1.0, S["xh1"])
                for c in range(DC):
                    act.wait_ge(S["q1_ready"], 2 * b + (c + 1))
                    if c:
                        act.wait_ge(S["q1_evac"], 2 * b + 1)
                    a.activation(qh[:, c, :], ps[:, 2 + c, :], ACT.Identity, bias=ba1[:, 1, c:c + 1], scale=WS / 4 / (XS * WS))
                    a.activation(q32, ps[:, 2 + c, :], ACT.Identity, bias=ba1[:, 1, c:c + 1],
                                 scale=WS / 4 / (XS * WS)).then_inc(S["qh1"], 1)
                split_weights(1, b, 0)
                for j in range(TB):
                    act.wait_ge(S["score1_shifted"], TB * b + (j + 1))
                    a.activation(es, es, ACT.Exp, scale=1.0 / (WS * WS)).then_inc(S["exp1_ready"], 1)
                    for h in range(2):
                        act.wait_ge(S["exp1_turned"], 2 * TB * b + (2 * j + h + 1))
                        hi(eth[:, 4 * h:4 * h + 4, :], ps[:, 6 + h, :], PS, S["eh1"])
                for h in range(2):
                    act.wait_ge(S["ctx1_turned"], 2 * b + (h + 1))
                    hi(xth[:, 2 * h:2 * h + 2], ps[:, h, :], WS, S["ch1"])
                split_weights(1, b, 1)
                logits_turn(1, b)
            with act.Fori(0, NB) as b:
                attention1(b)
            gate_weights(1)
            experts(1)

        @block.vector
        def _(dve):
            v = nc.vector
            own = Done(dve, S["dve_order"])

            def norm(base, dst, done):
                dve.sem_inc(S["dve_turn"], 1)
                for j in range(TB):
                    own.add(v.bn_stats(stats[:, j, :], X[:, ds(base + j * D, D)]))
                own.wait()
                own.add(v.tensor_tensor(mean[:], stats[:, :, 1], stats[:, :, 4], ALU.add))
                own.add(v.tensor_tensor(lt[:], stats[:, :, 1], stats[:, :, 4], ALU.subtract))
                own.add(v.tensor_tensor(ve[:], stats[:, :, 2], stats[:, :, 5], ALU.add))
                own.wait()
                own.add(v.scalar_tensor_tensor(out=lt[:], in0=lt[:], scalar=0.25, in1=lt[:], op0=ALU.mult, op1=ALU.mult))
                own.add(v.tensor_scalar(mean[:], mean[:], 0.5, None, ALU.mult))
                own.wait()
                own.add(v.scalar_tensor_tensor(out=ve[:], in0=ve[:], scalar=1.0 / D, in1=lt[:], op0=ALU.mult, op1=ALU.add))
                own.wait()
                own.add(v.tensor_scalar(ve[:], ve[:], EPS, 1.0 / XS / XS, ALU.add, ALU.mult))
                own.wait()
                own.add(v.tensor_scalar(rstd[:].bitcast(I32), ve[:].bitcast(I32), 1, None, ALU.logical_shift_right))
                own.wait()
                own.add(v.tensor_scalar(rstd[:].bitcast(I32), rstd[:].bitcast(I32), -1.0, RSQRT_SEED, ALU.mult, ALU.add))
                own.wait()
                for _ in range(3):
                    own.add(v.tensor_tensor(lt[:], rstd[:], rstd[:], ALU.mult))
                    own.wait()
                    own.add(v.scalar_tensor_tensor(out=lt[:], in0=lt[:], scalar=-0.5, in1=ve[:], op0=ALU.mult, op1=ALU.mult))
                    own.wait()
                    own.add(v.scalar_tensor_tensor(out=rstd[:], in0=lt[:], scalar=1.5, in1=rstd[:], op0=ALU.add, op1=ALU.mult))
                    own.wait()
                for j in range(TB):
                    last = v.tensor_scalar(dst[:, j, 0:D], X[:, ds(base + j * D, D)], mean[:, j:j + 1], rstd[:, j:j + 1],
                                           ALU.subtract, ALU.mult)
                last.then_inc(done, 1)

            def lo(dst, src, scale, hi_part, done):
                v.scalar_tensor_tensor(out=dst, in0=src, scalar=scale, in1=hi_part, op0=ALU.mult, op1=ALU.subtract).then_inc(done, 1)

            def split_weights(l, e, h):
                dve.wait_ge(w_hi[l], 2 * e + (h + 1))
                lo(wlo(l, e, h * HALF[l], HALF[l]), stage[:, h, 0:HALF[l]], WS, whi(l, e, h * HALF[l], HALF[l]), w_lo[l])

            dve.wait_ge(S["consts_ready"], 1)
            dve.wait_ge(S["prep0_in"], 160)
            dve.wait_ge(S["tanh_ready"], 1)
            own.add(v.tensor_copy(fill[:], region0[:]))
            own.add(v.tensor_scalar(tgs[:, 0:1], tg[:, 0:1], 1.0 / (XS * WS), None, ALU.mult))
            own.add(v.tensor_scalar(tgs[:, 1:2], tg[:, 2:3], 1.0 / (WS * WS), None, ALU.mult))
            dve.wait_ge(S["x_in0"], 16)
            norm(0, xn, S["norm0_ready"])
            own.add(v.memset(smw[:, :, KEYS:P], 0.0))
            own.add(v.memset(vwh[KEYS:P], 0.0))
            own.add(v.memset(vwl[KEYS:P], 0.0))
            for half, dst in ((0, kt0), (1, vt0)):
                dve.wait_ge(S["k0v0_ready"], half + 1)
                for c in range(DC):
                    last = v.tensor_scalar(dst[:, c, :], ps[:, 2 * half + c, :], ba0[:, half, c:c + 1], None, ALU.add)
                last.then_inc(S["k0_copied"], 1)

            def split_ps(h, l_, src, scale):
                own.add(v.tensor_scalar(h, src, scale, None, ALU.mult))
                own.wait()
                own.add(v.scalar_tensor_tensor(out=l_, in0=src, scalar=scale, in1=h, op0=ALU.mult, op1=ALU.subtract))
            split_ps(wo0h, wo0l, wa0[3], WS)
            split_ps(rth[:], rtl[:], rts[:, 0], WS)
            dve.wait_ge(S["g0_ready"], 1)
            for c in range(DC):
                split_ps(gh[:, c, :], gl[:, c, :], ps[:, 4 + c, :], WS / D ** 0.5)
            split_ps(cbh, cbl, ps[0:1, 6, :], WS / D ** 0.5)
            own.wait()
            dve.sem_inc(S["g0_copied"], 1)
            for q in range(4):
                dve.wait_ge(S["vw0_ready"], q + 1)
                split_ps(vwh[0:KEYS, 2 * q:2 * q + 2, :], vwl[0:KEYS, 2 * q:2 * q + 2, :],
                         ps[0:KEYS, q, :].rearrange("p (a b) -> p a b", a=2), WS)
            own.wait()
            dve.sem_inc(S["w0_split"], 1)
            dve.wait_ge(S["x_in"], 16)

            def tail(l, b, gate_col):
                for h in range(2):
                    dve.wait_ge(S[f"attn{l}_ready"], 2 * b + (h + 1))
                    dve.sem_inc(S["dve_turn"], 1)
                    for i in range(2):
                        at = X[:, ds(b * (TB * D) + (2 * h + i) * D, D)]
                        own.add(v.scalar_tensor_tensor(out=at, in0=ps[:, O_BANK[l] + h, i * D:(i + 1) * D], scalar=tgs[:, gate_col:gate_col + 1],
                                                       in1=at, op0=ALU.mult, op1=ALU.add))
                own.wait()
                dve.wait_ge(S[f"rows{l}_sent"], 2 * TB * 16 * b + 16)
                norm(b * (TB * D), xnr, S[f"lg_norm{l}"])
                for h in range(2):
                    dve.wait_ge(S[f"lg_xh{l}"], 2 * b + (h + 1))
                    lo(xtl[:, 2 * h:2 * h + 2], ps[:, h, :], 1.0, xth[:, 2 * h:2 * h + 2], S[f"lg_xl{l}"])

            def route(l, b):
                dve.wait_ge(S[f"logits{l}_ready"], b + 1)
                own.add(v.tensor_copy(logit[:], ps[:, 6, 0:TB * E].rearrange("p (a b) -> p a b", a=TB)))
                own.wait()
                for k, m in ((0, m1), (1, m2)):
                    own.add(v.tensor_reduce(m[:], logit[:], axis=AX, op=ALU.max))
                    own.wait()
                    own.add(v.tensor_tensor(eq[:], logit[:], spread(m[:], 2, (P, TB, E)), ALU.is_equal))
                    own.wait()
                    own.add(v.tensor_tensor(eq[:], eq[:], revidx[:], ALU.mult))
                    own.wait()
                    own.add(v.tensor_reduce(mi[:, k, :], eq[:], axis=AX, op=ALU.max))
                    own.wait()
                    own.add(v.tensor_tensor(oh[:, k], eq[:], spread(mi[:, k, :], 2, (P, TB, E)), ALU.is_equal))
                    own.wait()
                    if k == 0:
                        own.add(v.scalar_tensor_tensor(out=logit[:], in0=oh[:, 0], scalar=FAR, in1=logit[:], op0=ALU.mult, op1=ALU.add))
                        own.wait()
                v.tensor_tensor(sel[:], oh[:, 0], oh[:, 1], ALU.add).then_inc(S[f"sel{l}_ready"], 1)
                own.add(v.tensor_tensor(dif[:, ds(b * TB, TB)], m2[:], m1[:], ALU.subtract))
                own.add(v.tensor_scalar(xnr[:, :, D:D + 1], tokid[:, ds(b * TB, TB)].unsqueeze(2), 0.0, None, ALU.add))
                own.add(v.tensor_copy(xnr[:, :, D + 1:D + 2], mi[:, 0, :].unsqueeze(2)))
                dve.wait_ge(S[f"count{l}_ready"], b + 1)
                own.add(v.tensor_tensor(posr[:], ps[:, 7, 0:TB * E].rearrange("p (a b) -> p a b", a=TB),
                                        spread(fill[:], 1, (P, TB, E)), ALU.add))
                own.wait()
                own.add(v.tensor_tensor(fill[:], ps[:, 7, TB * E:(TB + 1) * E], fill[:], ALU.add))
                own.add(v.tensor_tensor(pk[:], oh[:], spread(posr[:], 1, (P, 2, TB, E)), ALU.mult))
                own.wait()
                own.add(v.tensor_reduce(slot[:], pk[:].rearrange("p k t e -> p (k t) e"), axis=AX, op=ALU.add))
                own.wait()
                v.tensor_copy(sloti[:], slot[:]).then_inc(S[f"slots{l}_ready"], 1)

            def attention0(b, last_batch):
                for h in range(2):
                    dve.wait_ge(S["xh0"], 2 * b + (h + 1))
                    lo(xtl[:, 2 * h:2 * h + 2], ps[:, h, :], 1.0, xth[:, 2 * h:2 * h + 2], S["xl0"])
                dve.wait_ge(S["score0_ready"], b + 1)
                scores = ps[:, 2, 0:TB * KEYS].rearrange("p (a b) -> p a b", a=TB)
                own.add(v.tensor_reduce(m1[:], scores, axis=AX, op=ALU.max))
                own.wait()
                v.tensor_tensor(sm, scores, spread(m1[:], 2, (P, TB, KEYS)), ALU.subtract).then_inc(S["score0_shifted"], 1)
                if not last_batch:
                    split_weights(0, b, 0)
                dve.wait_ge(S["exp0_ready"], b + 1)
                own.add(v.tensor_reduce(m1[:], sm, axis=AX, op=ALU.add))
                own.wait()
                own.add(v.reciprocal(m2[:], m1[:]))
                own.wait()
                v.tensor_tensor(sm, sm, spread(m2[:], 2, (P, TB, KEYS)), ALU.mult).then_inc(S["prob0_ready"], 1)
                if not last_batch:
                    norm((b + 1) * (TB * D), xn, S["norm0_ready"])
                dve.wait_ge(S["ph0"], b + 1)
                lo(ptl, ps[:, 3, :].rearrange("p (a b) -> p a b", a=TB), PS, pth, S["pl0"])
                tail(0, b, 0)
                if not last_batch:
                    split_weights(0, b, 1)
                route(0, b)

            def repeat(n, per, body):
                start = own.base + own.n
                with dve.Fori(0, n) as b:
                    own.base, own.n = b * per + start, 0
                    body(b)
                    assert own.n == per, (own.n, per)
                own.base, own.n = start + n * per, 0
            repeat(NB - 1, STEPS0, lambda b: attention0(b, False))
            attention0(NB - 1, True)
            own.wait()

            def table(l):
                own.wait()
                dve.sem_inc(S[f"diff{l}_ready"], 1)
                own.add(v.tensor_scalar(padslot[:], fill[:], pcol[:], None, ALU.add))
                own.add(v.tensor_tensor(endA[:], fill[:], region0[:], ALU.subtract))
                own.wait()
                own.add(v.tensor_tensor(over, spread(endA[:], 2, (P, E, NT)), steps128[:], ALU.is_gt))
                own.wait()
                own.add(v.tensor_reduce(tiles[:], over, axis=AX, op=ALU.add))
                own.wait()
                own.add(v.tensor_copy(endA[:], tiles[:]))
                own.wait()
                src, dst = endA, endB
                for step in (1, 2, 4):
                    own.add(v.tensor_copy(dst[:, 0:step], src[:, 0:step]))
                    own.add(v.tensor_tensor(dst[:, step:E], src[:, step:E], src[:, 0:E - step], ALU.add))
                    own.wait()
                    src, dst = dst, src
                own.add(v.tensor_tensor(ended, spread(src[:], 1, (P, FT, E)), spread(tileno[:], 2, (P, FT, E)), ALU.is_le))
                own.wait()
                own.add(v.tensor_tensor(skipped, ended, spread(tiles[:], 1, (P, FT, E)), ALU.mult))
                own.add(v.tensor_reduce(nended, ended, axis=AX, op=ALU.add))
                own.wait()
                own.add(v.tensor_reduce(tskip, skipped, axis=AX, op=ALU.add))
                own.add(v.tensor_scalar(code[:], nended, -1.0, float(E), ALU.mult, ALU.add))
                own.add(v.tensor_scalar(expert[:], nended, float(E - 1), None, ALU.min))
                own.wait()
                own.add(v.tensor_tensor(tskip, tileno[:], tskip, ALU.subtract))
                own.add(v.tensor_scalar(nended, nended, float(REGION), None, ALU.mult))
                own.wait()
                own.add(v.scalar_tensor_tensor(out=tskip, in0=tskip, scalar=float(P), in1=nended, op0=ALU.mult, op1=ALU.add))
                own.wait()
                own.add(v.tensor_scalar(rowbase[:], tskip, float(E * REGION), None, ALU.min))
                own.wait()
                dve.sem_inc(S[f"table{l}_ready"], 1)
                dve.wait_ge(S[f"e2{l}_ready"], 1)
                own.add(v.tensor_scalar(wgt[:, 0, :], dif[:], 1.0, None, ALU.add))
                own.wait()
                own.add(v.reciprocal(wgt[:, 0, :], wgt[:, 0, :]))
                own.wait()
                own.add(v.tensor_scalar(wgt[:, 0, :], wgt[:, 0, :], tg[:, 2 * l + 1:2 * l + 2], None, ALU.mult))
                own.wait()
                own.add(v.tensor_tensor(wgt[:, 1, :], wgt[:, 0, :], dif[:], ALU.mult))
                own.wait()

            def experts(l):
                f = F[l]
                dve.sem_inc(f["y_out"], 1)

                def xlo(t):
                    dve.wait_ge(f["xh"], t + 1)
                    lo(fxl, ps[:, 0, 0:D].rearrange("p (a b) -> p a b", a=DC), 1.0, fxh, f["xl"])

                def ids(t, half, parity):
                    dve.wait_ge(f[f"row_in{parity}"], 16 * half + 16)
                    dve.wait_ge(f[f"sent{parity}"], 16 * half + 16)
                    dve.sem_inc(S["dve_turn"], 1)
                    own.add(v.tensor_tensor(idt[:, 0:1], row_in[:, parity, D + 1:D + 2], code[:, ds(t, 1)], ALU.not_equal))
                    own.wait()
                    v.scalar_tensor_tensor(out=idc[:, parity:parity + 1], in0=idt[:, 0:1], scalar=float(TOKENS),
                                           in1=row_in[:, parity, D:D + 1], op0=ALU.mult, op1=ALU.add).then_inc(f["ids"], 1)

                def product(t, first):
                    if l:
                        dve.wait_ge(f["h_ready"], 2 * t + 2)
                        dve.wait_ge(f["act_done"], t + 1)
                        if not first:
                            dve.wait_ge(f["g_turned"], t)
                        v.scalar_tensor_tensor(out=g32[:, 0:512], in0=ps[:, 2, :], scalar=1.0 / (XS * WS), in1=s32,
                                               op0=ALU.mult, op1=ALU.mult).then_inc(f["g_ready"], 1)

                def result(t, parity):
                    dve.wait_ge(f["y_ready"], t + 1)
                    v.tensor_scalar(y32[:, parity, :], ps[:, 5, 0:D], 1.0 / (HS * WS), None, ALU.mult).then_inc(f["y_out"], 1)

                def glo(t):
                    for h in range(2 - l):
                        dve.wait_ge(f["gh"], (2 - l) * t + (h + 1))
                        lo(fgl[:, h * 512:(h + 1) * 512], ps[:, 3 + h, :], HS, fgh[:, h * 512:(h + 1) * 512], f["gl"])

                def turn(t, half, parity):
                    product(t, False)
                    xlo(t + 1)
                    result(t - 1, 1 - parity)
                    ids(t, half, parity)
                    glo(t)
                xlo(0)
                product(0, True)
                xlo(1)
                ids(0, 0, 0)
                glo(0)
                start = own.base + own.n
                with dve.Fori(0, (FT - 2) // 2) as m:
                    own.base, own.n = 2 * m + start, 0
                    turn(2 * m + 1, m, 1)
                    turn(2 * m + 2, m + 1, 0)
                own.base, own.n = start + 2 * ((FT - 2) // 2), 0
                for t in range(1 + 2 * ((FT - 2) // 2), FT - 1):
                    turn(t, t // 2, t % 2)
                t = FT - 1
                product(t, False)
                result(t - 1, 1 - t % 2)
                ids(t, t // 2, t % 2)
                glo(t)
                result(t, t % 2)

            def combine(l, done):
                dve.sem_inc(back_used[l], 4)
                start = own.base + own.n
                with dve.Fori(0, NB // 4) as m:
                    own.base, own.n = m * (4 * 2 * TB) + start, 0
                    for r in range(4):
                        dve.wait_ge(back_in[l][r], 32 * m + 32)
                        dve.sem_inc(S["dve_turn"], 1)
                        for k in range(2):
                            for j in range(TB):
                                at = X[:, ds(m * (4 * TB * D) + (r * TB + j) * D, D)]
                                own.add(v.scalar_tensor_tensor(out=at, in0=back[r][k][:, j, :],
                                                               scalar=wgt[:, k, ds(m * (4 * TB) + (r * TB + j), 1)],
                                                               in1=at, op0=ALU.mult, op1=ALU.add))
                            own.wait()
                        dve.sem_inc(back_used[l], 1)
                        if done:
                            dve.sem_inc(done, 1)
                own.base, own.n = start + NB * 2 * TB, 0

            table(0)
            for h in range(2):
                split_weights(0, E - 1, h)
            experts(0)
            combine(0, None)

            dve.wait_ge(S["prep1_in"], 16 * 8)
            norm(0, xn, S["norm1_ready"])
            split_ps(wq1h, wq1l, wq1, WS)
            split_ps(wo1h, wo1l, wo1, WS)
            split_ps(bo1h, bo1l, bo1s, WS * WS / XS)
            split_ps(rth[:], rtl[:], rts[:, 1], WS)
            own.add(v.tensor_scalar(ba1[:, 1, :], ba1[:, 1, :], WS / 4, None, ALU.mult))
            own.add(v.tensor_copy(fill[:], region0[:]))
            for c in range(DC):
                dve.wait_ge(S["kv1_ready"], c + 1)
                own.add(v.tensor_scalar(q32, ps[:, 2 + c, :], ba1[:, 0, c:c + 1], None, ALU.add))
                own.wait()
                split_ps(kt1h[:, c, :], kt1l[:, c, :], q32, WS)
                own.wait()
            dve.sem_inc(S["w1_split"], 1)
            for q in range(4):
                dve.wait_ge(S["kv1_ready"], DC + q + 1)
                v.tensor_copy(v1[:, 2 * q:2 * q + 2, :], ps[:, 4 + q, :].rearrange("p (a b) -> p a b", a=2)).then_inc(S["kv1_copied"], 1)
            own.add(v.memset(vbl[:, :, 32:34], 0.0))
            own.add(v.tensor_scalar(vbh[:, :, 32:34], spread(smask[:], 1, (P, PAIRS, 2)), WS, None, ALU.mult))
            own.wait()
            dve.wait_ge(S["kv1_copied"], 4)

            def attention1(b, last_batch):
                for h in range(2):
                    dve.wait_ge(S["xh1"], 2 * b + (h + 1))
                    lo(xtl[:, 2 * h:2 * h + 2], ps[:, h, :], 1.0, xth[:, 2 * h:2 * h + 2], S["xl1"])
                dve.sem_inc(S["dve_turn"], 1)
                for c in range(DC):
                    for dst, src in ((kbh, kt1h), (kbl, kt1l)):
                        v.tensor_tensor(dst[:, c, :].rearrange("p (h k) -> p h k", h=HPC),
                                        spread(src[:, c, ds(b * KEYS, KEYS)], 1, (P, HPC, KEYS)),
                                        spread(hmask[:], 2, (P, HPC, KEYS)), ALU.mult).then_inc(S["kb1_ready"], 1)
                own.add(v.tensor_tensor(vb32.rearrange("p a (s f) -> p a s f", s=2),
                                        v1[:, ds(b, 1), :].rearrange("p o (a s f) -> p (o a) s f", a=PAIRS, s=2),
                                        smask[:].unsqueeze(1).unsqueeze(3).broadcast_to((P, PAIRS, 2, HD)), ALU.mult))
                own.wait()
                own.add(v.tensor_scalar(vbh[:, :, 0:32], vb32, WS, None, ALU.mult))
                own.wait()
                v.scalar_tensor_tensor(out=vbl[:, :, 0:32], in0=vb32, scalar=WS, in1=vbh[:, :, 0:32],
                                       op0=ALU.mult, op1=ALU.subtract).then_inc(S["kb1_ready"], 1)
                for c in range(DC):
                    dve.wait_ge(S["qh1"], 2 * b + (c + 1))
                    v.tensor_tensor(ql[:, c, :], q32, qh[:, c, :], ALU.subtract).then_inc(S["q1_evac"], 1)
                split_weights(1, b, 0)

                def shift(j):
                    dve.wait_ge(S["score1_ready"], TB * b + (j + 1))
                    s0 = S_BANK[j % 2]
                    scores = ps[:, s0:s0 + 2, :].rearrange("p a (h k) -> p (a h) k", k=KEYS)
                    own.add(v.tensor_reduce(m16[:], scores, axis=AX, op=ALU.max))
                    own.wait()
                    if j:
                        dve.wait_ge(S["exp1_turned"], 2 * TB * b + 2 * j)
                    v.tensor_tensor(es.rearrange("p (h k) -> p h k", k=KEYS), scores, spread(m16[:], 2, (P, HEADS, KEYS)),
                                    ALU.subtract).then_inc(S["score1_shifted"], 1)

                def elo(j):
                    for h in range(2):
                        dve.wait_ge(S["eh1"], 2 * TB * b + (2 * j + h + 1))
                        lo(etl[:, 4 * h:4 * h + 4, :], ps[:, 6 + h, :].rearrange("p (a b) -> p a b", a=4), PS,
                           eth[:, 4 * h:4 * h + 4, :], S["el1"])

                def context(j):
                    dve.wait_ge(S["pv1_ready"], TB * b + (j + 1))
                    pv = ps[:, j % 2, 0:PAIRS * 34].rearrange("p (a c) -> p a c", c=34)
                    own.add(v.reciprocal(r16[:], pv[:, :, 32:34]))
                    own.wait()
                    v.tensor_tensor(xn[:, j, :].rearrange("p (a s f) -> p a s f", a=PAIRS, s=2),
                                    pv[:, :, 0:32].rearrange("p a (s f) -> p a s f", s=2),
                                    spread(r16[:], 3, (P, PAIRS, 2, HD)), ALU.mult).then_inc(S["ctx1_ready"], 1)
                shift(0)
                for j in range(TB):
                    elo(j)
                    if j + 1 < TB:
                        shift(j + 1)
                    context(j)
                for h in range(2):
                    dve.wait_ge(S["ch1"], 2 * b + (h + 1))
                    lo(xtl[:, 2 * h:2 * h + 2], ps[:, h, :], WS, xth[:, 2 * h:2 * h + 2], S["cl1"])
                if not last_batch:
                    norm((b + 1) * (TB * D), xn, S["norm1_ready"])
                tail(1, b, 1)
                split_weights(1, b, 1)
                route(1, b)
            repeat(NB - 1, STEPS1, lambda b: attention1(b, False))
            attention1(NB - 1, True)
            table(1)
            experts(1)
            combine(1, S["out_ready"])

        @block.tensor
        def _(pe):
            mm = nc.tensor.matmul

            def turn4(src, done):
                for j in range(TB):
                    for c in range(DC):
                        at = (j % 2) * D + c * P
                        last = nc.tensor.transpose(ps[:, j // 2, at:at + P], src[:, j, c * P:(c + 1) * P], ident[:])
                    if j % 2:
                        last.then_inc(done, 1)

            def passes(dst, left, right, start=True, stop=True):
                n = len(left)
                for i in range(n):
                    for q, (a_, b_) in enumerate(rh_rl):
                        last = mm(dst, left[i][a_], right[i][b_], start=start and i == 0 and q == 0,
                                  stop=stop and i == n - 1 and q == 2)
                return last

            def tail(l, b):
                pe.wait_ge(S[f"lg_norm{l}"], b + 1)
                turn4(xnr, S[f"lg_turned{l}"])
                for h in range(2):
                    pe.wait_ge(S[f"lg_xl{l}"], 2 * b + (h + 1))
                    for j in (2 * h, 2 * h + 1):
                        last = passes(ps[:, 6, j * E:(j + 1) * E], [(xth[:, j, c, :], xtl[:, j, c, :]) for c in range(DC)],
                                      [(rth[:, c, :], rtl[:, c, :]) for c in range(DC)])
                last.then_inc(S[f"logits{l}_ready"], 1)
                pe.wait_ge(S[f"sel{l}_ready"], b + 1)
                s2 = sel[:].rearrange("p a b -> p (a b)")
                mm(ps[:, 7, 0:TB * E], before[:], s2, start=True, stop=False)
                for j in range(1, TB):
                    mm(ps[:, 7, j * E:TB * E], ones16[:], s2[:, 0:(TB - j) * E], start=False, stop=False)
                for j in range(TB):
                    last = mm(ps[:, 7, TB * E:(TB + 1) * E], ones16[:], s2[:, j * E:(j + 1) * E], start=False, stop=j == TB - 1)
                last.then_inc(S[f"count{l}_ready"], 1)

            pe.wait_ge(S["consts_ready"], 1)
            pe.wait_ge(S["prep0_in"], 160)
            for half in range(2):
                for c in range(DC):
                    for k in range(DC):
                        last = mm(ps[:, 2 * half + c, :], wa0[half][:, k, c * P:(c + 1) * P], ctx0[:, k, :], start=k == 0, stop=k == DC - 1)
                last.then_inc(S["k0v0_ready"], 1)
            pe.wait_ge(S["k0_copied"], 1)
            for c in range(DC):
                for k in range(DC):
                    mm(ps[:, 4 + c, :], wa0[2][:, k, c * P:(c + 1) * P], kt0[:, k, :], start=k == 0, stop=k == DC - 1)
            for k in range(DC):
                last = mm(ps[0:1, 6, :], ba0[:, 2, k:k + 1], kt0[:, k, :], start=k == 0, stop=k == DC - 1)
            last.then_inc(S["g0_ready"], 1)
            pe.wait_ge(S["k0_copied"], 2)
            for b in range(NB):
                dst = ps[:, b // 2, (b % 2) * D:(b % 2 + 1) * D]
                for k in range(DC):
                    mm(dst[0:KEYS, :], vt0[:, k, b * KEYS:(b + 1) * KEYS], wa0[3][:, k, :], start=k == 0, stop=False)
                last = mm(dst[0:KEYS, :], onesf[:, 0:KEYS], bo0s, start=False, stop=True)
                if b % 2:
                    last.then_inc(S["vw0_ready"], 1)
            pe.wait_ge(S["w0_split"], 1)

            def attention0(b):
                pe.wait_ge(S["norm0_ready"], b + 1)
                turn4(xn, S["turned0"])
                for j in range(TB):
                    if j % 2 == 0:
                        pe.wait_ge(S["xl0"], 2 * b + (j // 2 + 1))
                    dst = ps[:, 2, j * KEYS:(j + 1) * KEYS]
                    passes(dst, [(xth[:, j, c, :], xtl[:, j, c, :]) for c in range(DC)],
                           [(gh[:, c, ds(b * KEYS, KEYS)], gl[:, c, ds(b * KEYS, KEYS)]) for c in range(DC)], stop=False)
                    mm(dst, rowscale[:], cbh[:, ds(b * KEYS, KEYS)], start=False, stop=False)
                    last = mm(dst, rowscale[:], cbl[:, ds(b * KEYS, KEYS)], start=False, stop=True)
                last.then_inc(S["score0_ready"], 1)
                pe.wait_ge(S["prob0_ready"], b + 1)
                for j in range(TB):
                    last = nc.tensor.transpose(ps[:, 3, j * P:(j + 1) * P], smw[:, j, :], ident[:])
                last.then_inc(S["prob0_turned"], 1)
                pe.wait_ge(S["pl0"], b + 1)
                pe.sem_inc(S["pe_turn"], 1)
                for j in range(TB):
                    dst = ps[:, O_BANK[0] + j // 2, (j % 2) * D:(j % 2 + 1) * D]
                    passes(dst, [(xth[:, j, c, :], xtl[:, j, c, :]) for c in range(DC)],
                           [(wo0h[:, c, :], wo0l[:, c, :]) for c in range(DC)], stop=False)
                    last = passes(dst, [(pth[:, j, :], ptl[:, j, :])], [(vwh[:, ds(b, 1), :], vwl[:, ds(b, 1), :])], start=False)
                    if j % 2:
                        last.then_inc(S["attn0_ready"], 1)
                tail(0, b)
            with pe.Fori(0, NB) as b:
                attention0(b)

            def experts(l):
                f = F[l]
                n = 2 - l

                def A(t, half, parity):
                    pe.wait_ge(f[f"row_in{parity}"], 16 * half + 16)
                    for c in range(DC):
                        last = nc.tensor.transpose(ps[:, 0, c * P:(c + 1) * P], row_in[:, parity, c * P:(c + 1) * P], ident[:])
                    last.then_inc(f["turned"], 1)

                def B(t, e, first):
                    pe.wait_ge(f["xl"], t + 1)
                    for h in range(2):
                        if not first:
                            pe.wait_ge(f["act_done"], 2 * t + (h - 1)) if l == 0 else pe.wait_ge(f["g_ready"], t)
                        last = passes(ps[:, 1 + h, :], [(fxh[:, c, :], fxl[:, c, :]) for c in range(DC)],
                                      [(whi(l, e, c * 1024 + h * 512, 512), wlo(l, e, c * 1024 + h * 512, 512)) for c in range(DC)])
                        last.then_inc(f["h_ready"], 1)

                def C(t):
                    for h in range(n):
                        pe.wait_ge(f["act_done"] if l == 0 else f["g_ready"], n * t + (h + 1))
                        for i in range(4):
                            at = h * 512 + i * P
                            last = nc.tensor.transpose(ps[:, 3 + h, i * P:(i + 1) * P], g32[:, at:at + P], ident[:])
                        last.then_inc(f["g_turned"], 1)

                def Dn(t, e):
                    pe.wait_ge(f["gl"], n * t + n)
                    pe.wait_ge(f["y_out"], t + 1)
                    last = passes(ps[:, 5, 0:D], [(fgh[:, k * P:(k + 1) * P], fgl[:, k * P:(k + 1) * P]) for k in range(KD[l])],
                                  [(whi(l, e, 2048 + k * D, D), wlo(l, e, 2048 + k * D, D)) for k in range(KD[l])])
                    last.then_inc(f["y_ready"], 1)

                def number(t):
                    return pe.value_load(expert[0:1, ds(t, 1)], min_val=0, max_val=E - 1)

                def turn(t, half, parity):
                    B(t, number(t), False)
                    A(t + 1, half + parity, 1 - parity)
                    Dn(t - 1, number(t - 1))
                    C(t)
                pe.wait_ge(S[f"table{l}_ready"], 1)
                pe.wait_ge(w_lo[l], 2 * E)
                A(0, 0, 0)
                B(0, number(0), True)
                A(1, 0, 1)
                C(0)
                with pe.Fori(0, (FT - 2) // 2) as m:
                    turn(2 * m + 1, m, 1)
                    turn(2 * m + 2, m + 1, 0)
                for t in range(1 + 2 * ((FT - 2) // 2), FT - 1):
                    turn(t, t // 2, t % 2)
                t = FT - 1
                B(t, number(t), False)
                Dn(t - 1, number(t - 1))
                C(t)
                Dn(t, number(t))
            experts(0)

            pe.wait_ge(S["prep1_in"], 16 * 8)
            for c in range(DC):
                for k in range(DC):
                    last = mm(ps[:, 2 + c, :], wk1[:, k, c * P:(c + 1) * P], ctx1[:, k, :], start=k == 0, stop=k == DC - 1)
                last.then_inc(S["kv1_ready"], 1)
            pe.wait_ge(F[0]["y_out"], FT + 1)
            for b in range(NB):
                dst = ps[:, 4 + b // 2, (b % 2) * D:(b % 2 + 1) * D]
                for r in range(2):
                    for k in range(DC):
                        mm(dst[64 * r:64 * r + 64, :], ctx1[:, k, b * KEYS:(b + 1) * KEYS], wv1[:, k, :], start=k == 0, stop=False)
                    last = mm(dst[64 * r:64 * r + 64, :], onesf[:, 0:KEYS], bv1s, start=False, stop=True)
                if b % 2:
                    last.then_inc(S["kv1_ready"], 1)
            pe.wait_ge(S["w1_split"], 1)
            pe.wait_ge(S["kv1_copied"], 4)

            def attention1(b):
                pe.wait_ge(S["norm1_ready"], b + 1)
                turn4(xn, S["turned1"])
                pe.wait_ge(S["xl1"], 2 * b + 2)
                for c in range(DC):
                    passes(ps[:, 2 + c, :], [(wq1h[:, k, c * P:(c + 1) * P], wq1l[:, k, c * P:(c + 1) * P]) for k in range(DC)],
                           [(xth[:, :, k, :], xtl[:, :, k, :]) for k in range(DC)]).then_inc(S["q1_ready"], 1)
                pe.wait_ge(S["q1_evac"], 2 * b + 2)
                pe.wait_ge(S["kb1_ready"], 5 * b + 5)

                def scores(j):
                    if j >= 2:
                        pe.wait_ge(S["score1_shifted"], TB * b + (j - 1))
                    for c in range(DC):
                        q = slice(j * P, (j + 1) * P)
                        last = passes(ps[:, S_BANK[j % 2] + c, :], [(qh[:, c, q], ql[:, c, q])], [(kbh[:, c, :], kbl[:, c, :])])
                    last.then_inc(S["score1_ready"], 1)

                def exps(j):
                    pe.wait_ge(S["exp1_ready"], TB * b + (j + 1))
                    for h in range(2):
                        if j:
                            pe.wait_ge(S["el1"], 2 * TB * b + (2 * j - 1 + h))
                        for i in range(4):
                            at = (4 * h + i) * P
                            last = nc.tensor.transpose(ps[:, 6 + h, i * P:(i + 1) * P], es[:, at:at + P], ident[:])
                        last.then_inc(S["exp1_turned"], 1)

                def values(j):
                    pe.wait_ge(S["el1"], 2 * TB * b + (2 * j + 2))
                    if j >= 2:
                        pe.wait_ge(S["ctx1_ready"], TB * b + (j - 1))
                    for a_ in range(PAIRS):
                        last = passes(ps[:, j % 2, a_ * 34:(a_ + 1) * 34], [(eth[:, a_, :], etl[:, a_, :])], [(vbh[:, a_, :], vbl[:, a_, :])])
                    last.then_inc(S["pv1_ready"], 1)
                scores(0)
                for j in range(TB):
                    if j + 1 < TB:
                        scores(j + 1)
                    exps(j)
                    values(j)
                pe.wait_ge(S["ctx1_ready"], TB * b + TB)
                turn4(xn, S["ctx1_turned"])
                for j in range(TB):
                    if j % 2 == 0:
                        pe.wait_ge(S["cl1"], 2 * b + (j // 2 + 1))
                    dst = ps[:, O_BANK[1] + j // 2, (j % 2) * D:(j % 2 + 1) * D]
                    passes(dst, [(xth[:, j, c, :], xtl[:, j, c, :]) for c in range(DC)],
                           [(wo1h[:, c, :], wo1l[:, c, :]) for c in range(DC)], stop=False)
                    mm(dst, rowscale[:], bo1h, start=False, stop=False)
                    last = mm(dst, rowscale[:], bo1l, start=False, stop=True)
                    if j % 2:
                        last.then_inc(S["attn1_ready"], 1)
                tail(1, b)
            with pe.Fori(0, NB) as b:
                attention1(b)
            experts(1)


def kernel(**inputs):
    import numpy as np
    import concourse.bacc as bacc
    from concourse.bass_utils import run_bass_kernel_spmd

    a = {k: np.asarray(v) for k, v in inputs.items()}

    def rows128(m):
        return np.ascontiguousarray(m.reshape(-1, P, *m.shape[1:]).swapaxes(0, 1))

    def expert_weights(firsts, second):
        up = np.concatenate(firsts, axis=2).reshape(E, DC, P, -1).transpose(2, 0, 1, 3).reshape(P, E, -1)
        down = second.reshape(E, -1, P, D).transpose(2, 0, 1, 3).reshape(P, E, -1)
        return np.ascontiguousarray(np.concatenate([up, down], axis=2))

    def columns(*vs):
        return np.ascontiguousarray(np.stack([v.reshape(DC, P).T for v in vs], axis=1))

    ins = {
        "x": a["x"].reshape(NT, P, D),
        "ctxT": rows128(a["ctx_1024"].reshape(NB * KEYS, D).T),
        "gates": np.ascontiguousarray(np.broadcast_to(
            np.stack([a["g_xattn"][0], a["g_ffn"][0], a["g_xattn"][1], a["g_ffn"][1]]), (P, 4))),
        "w_attn0": np.stack([rows128(m) for m in (a["L0_xattn_Wk"].T, a["L0_xattn_Wv"].T, a["L0_xattn_Wq"], a["L0_xattn_Wo"].T)]),
        "b_attn0": columns(a["L0_xattn_bk"], a["L0_xattn_bv"], a["L0_xattn_bq"]),
        "bo0": a["L0_xattn_bo"].reshape(1, D),
        "rt0": rows128(a["L0_ffn_router_w"].T),
        "w_attn1": np.stack([rows128(a[f"L1_xattn_W{n}"].reshape(D, D)) for n in "kvqo"]),
        "b_attn1": columns(a["L1_xattn_bk"].reshape(D), a["L1_xattn_bq"].reshape(D)),
        "bv1": a["L1_xattn_bv"].reshape(1, D),
        "bo1": a["L1_xattn_bo"].reshape(1, D),
        "rt1": rows128(a["L1_ffn_Wg"].T),
        "w_ffn0": expert_weights([a["L0_ffn_w1"]], a["L0_ffn_w2"]),
        "w_ffn1": expert_weights([a["L1_ffn_W1"].transpose(0, 2, 1), a["L1_ffn_W2"].transpose(0, 2, 1)],
                                 a["L1_ffn_W3"].transpose(0, 2, 1)),
    }
    nc = bacc.Bacc("TRN2", target_bir_lowering=False, num_devices=1)
    args = {k: nc.dram_tensor(f"in_{k}", m.shape, mybir.dt.from_np(m.dtype), kind="ExternalInput").ap() for k, m in ins.items()}
    out = nc.dram_tensor("out", (NT, P, D), F32, kind="ExternalOutput").ap()
    build(nc, **args, out=out)
    r = run_bass_kernel_spmd(nc, [{f"in_{k}": m for k, m in ins.items()}], core_ids=[0])
    return r.results[0]["out"].reshape(NB, SEQ, D)
```

```python
from contextlib import ExitStack

import concourse.bass as bass
from concourse import mybir

F32 = mybir.dt.float32
F16 = mybir.dt.float16
I32 = mybir.dt.int32
ALU = mybir.AluOpType
ACT = mybir.ActivationFunctionType
AX = mybir.AxisListType.X
ds = bass.ds

P = 128
D = 256
DC = D // P
NB = 8
SEQ = 512
TB = SEQ // P
NT = NB * TB
TOKENS = NT * P
KEYS = 64
HEADS = 16
HD = D // HEADS
HPC = HEADS // DC
PAIRS = HEADS // 2
E = 8
EPS = 1e-5
REGION = TOKENS + P
ROW = D + 2
FT = (2 * TOKENS + E * (P - 1)) // P
PADROW = 2 * TOKENS
SLOTS = 4
UNROLL = SLOTS
TURNS = (FT - 2) // UNROLL
F0 = 4096
F1 = 3072

ARENA = 4368

XS = 2.0 ** 8
WS = 2.0 ** 6
HS = 2.0 ** 4
PS = 2.0 ** 8
FAR = -3.0e38
O_BANK = (4, 2)
T_BANK = (0, 6)
LOGITS_BANK = (6, 0)
COUNTS_BANK = (7, 0)
S_BANK = (4, 2)
STEPS0, STEPS1 = 51, 58
RSQRT_SEED = 1597463007.0


def build(nc, x, ctxT, gates, w_attn0, b_attn0, bo0, rt0, w_attn1, b_attn1, bv1, bo1, rt1, w_ffn0, w_ffn1, out):
    rows_dram = nc.dram_tensor("expert_rows", (E * REGION + P, ROW), F32, kind="Internal").ap()
    back_dram = nc.dram_tensor("token_rows", (PADROW + TOKENS + P, D), F32, kind="Internal").ap()

    with ExitStack() as stack:
        def sb(name, shape, dt=F32):
            return stack.enter_context(nc.sbuf_tensor(name, shape, dt))

        def sem(name):
            return stack.enter_context(nc.semaphore(name))

        W = sb("W", [P, E * 2 * F0], F16)
        X = sb("X", [P, NT * D])
        stage = sb("stage", [P, 2, F0 // 2])
        arena = sb("arena", [P, ARENA])
        ident = sb("ident", [P, P])
        before = sb("before", [P, P], F16)
        ones16 = sb("ones16", [P, P], F16)
        rowscale = sb("rowscale", [1, P], F16)
        onesf = sb("onesf", [1, P])
        revidx = sb("revidx", [P, TB, E])
        region0 = sb("region0", [P, E])
        steps128 = sb("steps128", [P, E, NT])
        tileno = sb("tileno", [P, FT])
        tokid = sb("tokid", [P, NT])
        padrow = sb("padrow", [P, ROW])
        hmask = sb("hmask", [P, HPC], F16)
        smask = sb("smask", [P, 2])
        xnr = sb("xnr", [P, TB, ROW])
        stats = sb("stats", [P, 2 * TB, 6])
        mean = sb("mean", [P, 2 * TB])
        rstd = sb("rstd", [P, 2 * TB])
        lt = sb("lt", [P, 2 * TB])
        shiftn = sb("shiftn", [P, 2 * TB])
        ve = sb("ve", [P, 2 * TB])
        tg = sb("tg", [P, 4])
        tgs = sb("tgs", [P, 2])
        gates_sb = sb("gates_sb", [P, 4])
        logit = sb("logit", [P, TB, E])
        eq = sb("eq", [P, TB, E])
        oh = sb("oh", [P, 2, TB, E])
        sel = sb("sel", [P, TB, E], F16)
        m1 = sb("m1", [P, TB])
        m2 = sb("m2", [P, TB])
        mi = sb("mi", [P, 2, TB])
        posr = sb("posr", [P, TB, E])
        pk = sb("pk", [P, 2, TB, E])
        slot = sb("slot", [P, 2 * TB])
        sloti = sb("sloti", [P, 2 * TB], I32)
        sloti_last = sb("sloti_last", [P, 2 * TB], I32)
        fill = sb("fill", [P, E])
        dif = sb("dif", [P, NT])
        wgt = sb("wgt", [P, 2, NT])
        tiles = sb("tiles", [P, E])
        endA = sb("endA", [P, E])
        endB = sb("endB", [P, E])
        code = sb("code", [P, FT])
        rowbase = sb("rowbase", [P, FT], I32)
        expert = sb("expert", [P, FT], I32)
        packed = sb("packed", [P, TURNS], I32)
        packing = sb("packing", [P, TURNS])
        fill_end = sb("fill_end", [P, E], I32)
        rth = sb("rth", [P, DC, E], F16)
        rtl = sb("rtl", [P, DC, E], F16)
        rts = sb("rts", [P, 2, DC, E])
        idc = sb("idc", [P, 2], I32)
        idt = sb("idt", [P, 2])
        ba1 = sb("ba1", [P, 2, DC])
        m16 = sb("m16", [P, 2, HEADS])
        r16 = sb("r16", [P, PAIRS, 2])

        class Carver:
            def __init__(self, ap, size):
                self.ap, self.at, self.size = ap, 0, size

            def take(self, shape, dt=F32, parts=P):
                n = 1
                for s in shape:
                    n *= s
                words = n if dt == F32 else (n + 1) // 2
                v = self.ap[0:parts, self.at:self.at + words]
                self.at += words
                assert self.at <= self.size, (self.at, self.size)
                if dt != F32:
                    v = v.bitcast(dt)
                if len(shape) == 2:
                    v = v.rearrange("p (a b) -> p a b", a=shape[0])
                elif len(shape) == 3:
                    v = v.rearrange("p (a b c) -> p a b c", a=shape[0], b=shape[1])
                return v

        Wf = W[:, :].bitcast(F32)
        c = Carver(Wf[:, 7 * F0:8 * F0], F0)
        gh, gl = c.take([DC, NB * KEYS], F16), c.take([DC, NB * KEYS], F16)
        vwh, vwl = c.take([NB, D], F16), c.take([NB, D], F16)
        wo0h, wo0l = c.take([DC, D], F16), c.take([DC, D], F16)
        pth, ptl = c.take([TB, P], F16), c.take([TB, P], F16)
        c = Carver(Wf[:, 5 * F0:7 * F0], 2 * F0)
        ctx0 = c.take([DC, NB * KEYS])
        wa0 = [c.take([DC, D]) for _ in range(4)]
        kt0, vt0 = c.take([DC, NB * KEYS]), c.take([DC, NB * KEYS])
        ba0 = c.take([3, DC])
        bo0s = c.take([D], F32, 1)
        c = Carver(arena, ARENA)
        xn = c.take([TB, D])
        xth, xtl = c.take([TB, DC, P], F16), c.take([TB, DC, P], F16)
        after_xt = c.at
        smw = c.take([TB, P])
        sm = smw[:, :, 0:KEYS]
        cbh, cbl = c.take([NB * KEYS], F16, 1), c.take([NB * KEYS], F16, 1)
        lth0, ltl0 = c.take([TB, DC, P], F16), c.take([TB, DC, P], F16)
        c = Carver(arena, ARENA)
        xnr_last = c.take([TB, ROW])
        c = Carver(arena, ARENA)
        c.at = after_xt
        wq1h, wq1l = c.take([DC, D], F16), c.take([DC, D], F16)
        wo1h, wo1l = c.take([DC, D], F16), c.take([DC, D], F16)
        bo1h, bo1l = c.take([D], F16, 1), c.take([D], F16, 1)
        q32 = c.take([SEQ])
        lth1, ltl1 = (stage[:, i, F1 // 2:].bitcast(F16).rearrange("p (t c k) -> p t c k", t=TB, c=DC) for i in range(2))
        lth, ltl = (lth0, lth1), (ltl0, ltl1)
        c = Carver(Wf[:, E * F1:E * F0], E * (F0 - F1))
        es = c.take([HEADS * KEYS])
        eth, etl = c.take([PAIRS, P], F16), c.take([PAIRS, P], F16)
        kbh, kbl = c.take([DC, HPC * KEYS], F16), c.take([DC, HPC * KEYS], F16)
        vbh, vbl = c.take([PAIRS, 34], F16), c.take([PAIRS, 34], F16)
        kt1h, kt1l = c.take([DC, NB * KEYS], F16), c.take([DC, NB * KEYS], F16)
        v1 = c.take([NB, D])
        qh, ql = c.take([DC, SEQ], F16), c.take([DC, SEQ], F16)
        vb32 = c.take([PAIRS, 32])
        c = Carver(stage[:, :, :].rearrange("p a b -> p (a b)"), F0)
        ctx1 = c.take([DC, NB * KEYS])
        wk1, wv1, wq1, wo1 = (c.take([DC, D]) for _ in range(4))
        bv1s, bo1s = c.take([D], F32, 1), c.take([D], F32, 1)
        c = Carver(Wf[:, 5 * F1:8 * F1], 3 * F1)
        back = [[c.take([TB, D]) for _ in range(2)] for _ in range(4)]
        c = Carver(arena, ARENA)
        row_in = c.take([SLOTS, ROW])
        fxh, fxl = c.take([DC, P], F16), c.take([DC, P], F16)
        y32 = c.take([2, D])
        g32 = c.take([1024])
        fgh, fgl = c.take([1024], F16), c.take([1024], F16)
        s32 = c.take([512])
        c = Carver(arena, ARENA)
        c.at = TB * ROW
        over = c.take([E, NT])
        ended, skipped = c.take([FT, E]), c.take([FT, E])
        nended, tskip = c.take([FT]), c.take([FT])

        ps = stack.enter_context(nc.psum_tensor("ps", [P, 8, 512], F32))

        names = """consts_ready tanh_ready
            prep0_in k0v0_ready k0_copied g0_ready g0_copied vw0_ready w0_split
            x_in0 x_in coef0_ready norm0_ready turned0 xh0 xl0 score0_ready score0_shifted exp0_ready prob0_ready prob0_turned ph0 pl0
            attn0_ready lg_norm0 lg_turned0 lg_xh0 lg_xl0 logits0_ready sel0_ready count0_ready count0_taken slots0_ready rows0_sent
            fill0_ready table0_ready packed0_ready pads0_sent diff0_ready e20_ready
            prep1_in kv1_ready kv1_copied w1_split
            coef1_ready norm1_ready turned1 xh1 xl1 q1_ready q1_evac qh1 kb1_ready score1_ready score1_shifted exp1_ready exp1_turned eh1 el1
            pv1_ready ctx1_ready ctx1_turned ch1 cl1
            attn1_ready lg_norm1 lg_turned1 lg_xh1 lg_xl1 logits1_ready sel1_ready count1_ready count1_taken slots1_ready rows1_sent
            fill1_ready table1_ready packed1_ready pads1_sent diff1_ready e21_ready
            out_ready out_sent pool_order act_turn dve_turn pe_turn pool_turn dve_order""".split()
        S = {n: sem(n) for n in names}
        w_in = [[sem(f"w{l}_in{h}") for h in range(2)] for l in range(2)]
        w_hi = [sem(f"w{l}_hi") for l in range(2)]
        w_lo = [sem(f"w{l}_lo") for l in range(2)]
        back_in = [[sem(f"back{l}_in{r}") for r in range(4)] for l in range(2)]
        back_used = [sem(f"back{l}_used") for l in range(2)]
        F = [{n: sem(f"f{l}_{n}") for n in """row_in0 row_in1 row_in2 row_in3 turned xh xl ids h_ready act_done g_ready g_turned gh gl
              y_ready y_out sent0 sent1 own""".split()} for l in range(2)]

        rh_rl = ((0, 0), (1, 0), (0, 1))

        def spread(ap, axis, shape):
            return ap.unsqueeze(axis).broadcast_to(shape)

        def tok(t):
            return X[:, ds(t * D, D)]

        class Done:
            def __init__(self, eng, s):
                self.eng, self.s, self.base, self.n = eng, s, 0, 0

            def add(self, ins):
                self.n += 1
                ins.then_inc(self.s, 1)

            def wait(self):
                self.eng.wait_ge(self.s, self.base + self.n)

        FW = (F0, F1)
        HALF = (F0 // 2, F1 // 2)
        KD = (8, 4)

        def whi(l, e, at, n):
            return W[:, ds(e * (2 * FW[l]) + at, n)]

        def wlo(l, e, at, n):
            return W[:, ds(e * (2 * FW[l]) + (FW[l] + at), n)]

        block = stack.enter_context(nc.Block())

        @block.sync
        def _(sp):
            for dst, src in ((ctx0, ctxT), *((wa0[i], w_attn0[i]) for i in range(4)), (ba0, b_attn0), (bo0s, bo0),
                             (rts[:, 0], rt0), (rts[:, 1], rt1), (gates_sb[:], gates)):
                sp.dma_start(dst, src).then_inc(S["prep0_in"], 16)
            sp.dma_start(X[:, 0:2 * TB * D].rearrange("p (t d) -> p t d", t=2 * TB),
                         x[0:2 * TB].rearrange("t p d -> p t d")).then_inc(S["x_in0"], 16)
            sp.dma_start(X[:, 2 * TB * D:].rearrange("p (t d) -> p t d", t=NT - 2 * TB),
                         x[2 * TB:].rearrange("t p d -> p t d")).then_inc(S["x_in"], 16)

            def load_weights(l, src):
                for h in range(2):
                    sp.dma_start(stage[:, h, 0:HALF[l]], src[:, 0, h * HALF[l]:(h + 1) * HALF[l]]).then_inc(w_in[l][h], 16)
                with sp.Fori(1, E) as e:
                    for h in range(2):
                        sp.wait_ge(w_lo[l], 2 * e + (h - 1))
                        sp.dma_start(stage[:, h, 0:HALF[l]], src[:, ds(e, 1), h * HALF[l]:(h + 1) * HALF[l]].rearrange(
                            "p a n -> p (a n)")).then_inc(w_in[l][h], 16)

            def load_rows(l):
                sp.wait_ge(S[f"fill{l}_ready"], 1)
                for e in range(E):
                    at = sp.value_load(fill_end[0:1, e:e + 1], min_val=0, max_val=E * REGION - P)
                    sp.dma_start(rows_dram[ds(at, P), :], padrow[:]).then_inc(S[f"pads{l}_sent"], 16)
                sp.wait_ge(S[f"table{l}_ready"], 1)
                sp.wait_ge(S[f"rows{l}_sent"], 16 + 16 * 2 * NT)
                sp.wait_ge(S[f"pads{l}_sent"], 16 * E)

                def load(t, slot):
                    at = sp.value_load(rowbase[0:1, ds(t, 1)], min_val=0, max_val=E * REGION)
                    sp.dma_start(row_in[:, slot, :], rows_dram[ds(at, P), :]).then_inc(F[l][f"row_in{slot}"], 16)
                for t in range(SLOTS):
                    load(t, t)
                if l == 0:
                    sp.wait_ge(w_lo[0], 2 * E)
                    for dst, src in ((ctx1, ctxT), *((v, w_attn1[i]) for i, v in enumerate((wk1, wv1, wq1, wo1))),
                                     (ba1[:], b_attn1), (bv1s, bv1), (bo1s, bo1)):
                        sp.dma_start(dst, src).then_inc(S["prep1_in"], 16)

                def turn(t, slot):
                    sp.wait_ge(F[l]["turned"], t - (SLOTS - 1))
                    sp.wait_ge(F[l]["ids"], t - (SLOTS - 1))
                    load(t, slot)
                with sp.Fori(0, (FT - SLOTS) // SLOTS) as m:
                    for slot in range(SLOTS):
                        turn(SLOTS * m + (SLOTS + slot), slot)
                for t in range(FT - FT % SLOTS, FT):
                    turn(t, t % SLOTS)

            def load_back(l):
                for parity, n in ((0, (FT + 1) // 2), (1, FT // 2)):
                    sp.wait_ge(F[l][f"sent{parity}"], 16 + 16 * n)
                with sp.Fori(0, NB // 4) as m:
                    for r in range(4):
                        sp.wait_ge(back_used[l], 4 * m + (r + 1))
                        for k in range(2):
                            sp.dma_start(back[r][k], back_dram[ds(m * 4 * SEQ + (k * TOKENS + r * SEQ), SEQ), :].rearrange(
                                "(t p) d -> p t d", p=P)).then_inc(back_in[l][r], 16)

            load_weights(0, w_ffn0)
            load_rows(0)
            load_back(0)
            sp.wait_ge(S["w1_split"], 1)
            sp.wait_ge(S["kv1_ready"], DC + NB // 2)
            load_weights(1, w_ffn1)
            load_rows(1)
            load_back(1)

            with sp.Fori(0, NB) as b:
                sp.wait_ge(S["out_ready"], b + 1)
                sp.dma_start(out[ds(b * TB, TB)].rearrange("t p d -> p t d"),
                             X[:, ds(b * TB * D, TB * D)].rearrange("p (t d) -> p t d", t=TB)).then_inc(S["out_sent"], 16)
            sp.wait_ge(S["out_sent"], 16 * NB)

        @block.gpsimd
        def _(pool):
            own = Done(pool, S["pool_order"])
            g = nc.gpsimd
            own.add(g.memset(ident[:], 0.0))
            own.add(g.memset(before[:], 1.0))
            own.add(g.memset(ones16[:], 1.0))
            own.add(g.memset(rowscale[:], XS))
            own.add(g.memset(onesf[:], 1.0))
            own.add(g.memset(hmask[:], 1.0))
            own.add(g.memset(smask[:], 1.0))
            own.add(g.memset(padrow[:], 0.0))
            own.add(g.iota(revidx[:], [[0, TB], [-1, E]], base=E, channel_multiplier=0, allow_small_or_imprecise_dtypes=True))
            own.add(g.iota(region0[:], [[REGION, E]], base=0, channel_multiplier=0, allow_small_or_imprecise_dtypes=True))
            own.add(g.iota(steps128[:], [[0, E], [P, NT]], base=0, channel_multiplier=0, allow_small_or_imprecise_dtypes=True))
            own.add(g.iota(tileno[:], [[1, FT]], base=0, channel_multiplier=0, allow_small_or_imprecise_dtypes=True))
            own.add(g.iota(tokid[:], [[P, NT]], base=0, channel_multiplier=1, allow_small_or_imprecise_dtypes=True))
            own.wait()
            own.add(g.affine_select(ident[:], ident[:], pattern=[[-1, P]], compare_op=ALU.not_equal, fill=1.0, base=0, channel_multiplier=1))
            own.add(g.affine_select(before[:], before[:], pattern=[[1, P]], compare_op=ALU.is_ge, fill=0.0, base=-1, channel_multiplier=-1))
            own.add(g.affine_select(hmask[:], hmask[:], pattern=[[-HD, HPC]], compare_op=ALU.is_ge, fill=0.0, base=0, channel_multiplier=1))
            own.add(g.affine_select(smask[:], smask[:], pattern=[[-KEYS, 2]], compare_op=ALU.is_ge, fill=0.0, base=0, channel_multiplier=1))
            own.add(g.iota(padrow[:, D:D + 1], [[0, 1]], base=PADROW, channel_multiplier=1, allow_small_or_imprecise_dtypes=True))
            own.wait()
            own.add(g.affine_select(hmask[:], hmask[:], pattern=[[HD, HPC]], compare_op=ALU.is_ge, fill=0.0, base=HD - 1, channel_multiplier=-1))
            own.add(g.affine_select(smask[:], smask[:], pattern=[[KEYS, 2]], compare_op=ALU.is_ge, fill=0.0, base=KEYS - 1, channel_multiplier=-1))
            own.wait()
            pool.sem_inc(S["consts_ready"], 1)

            def scatter(dst, index, src, done):
                g.indirect_dma_start(dst, bass.IndirectOffsetOnAxis(ap=index, axis=0), src, None).then_inc(done, 16)

            for l in range(2):
                sent = S[f"rows{l}_sent"]
                pool.dma_start(rows_dram[E * REGION:E * REGION + P, :], padrow[:]).then_inc(sent, 16)

                def send_rows(b, rows, index):
                    pool.wait_ge(S[f"slots{l}_ready"], b + 1)
                    pool.sem_inc(S["pool_turn"], 1)
                    for j in range(TB):
                        for k in range(2):
                            scatter(rows_dram, index[:, k * TB + j:k * TB + j + 1], rows[:, j, :], sent)
                with pool.Fori(0, NB - 1) as b:
                    send_rows(b, xnr, sloti)
                send_rows(NB - 1, xnr_last, sloti_last)
                for parity in range(2):
                    pool.dma_start(back_dram[PADROW + (1 + parity) * P:PADROW + (2 + parity) * P, :],
                                   padrow[:, 0:D]).then_inc(F[l][f"sent{parity}"], 16)

                def send(t, half, parity):
                    pool.wait_ge(F[l]["y_out"], t + 2)
                    pool.wait_ge(F[l]["ids"], t + 1)
                    pool.wait_ge(F[l][f"sent{1 - parity}"], 16 * half + 16 * (1 + parity))
                    pool.sem_inc(S["pool_turn"], 1)
                    scatter(back_dram, idc[:, parity:parity + 1], y32[:, parity, :], F[l][f"sent{parity}"])
                with pool.Fori(0, FT // 2) as m:
                    for parity in range(2):
                        send(2 * m + parity, m, parity)
                if FT % 2:
                    send(FT - 1, FT // 2, 0)

        @block.scalar
        def _(act):
            a = nc.scalar

            def hi(dst, src, scale, done):
                a.activation(dst, src, ACT.Copy, scale=scale).then_inc(done, 1)

            def split_weights(l, e, h):
                act.wait_ge(w_in[l][h], 16 * e + 16)
                if l == 1:
                    act.wait_ge(F[0]["y_ready"], FT)
                act.sem_inc(S["act_turn"], 1)
                hi(whi(l, e, h * HALF[l], HALF[l]), stage[:, h, 0:HALF[l]], WS, w_hi[l])

            def logits_turn(l, b):
                for h in range(2):
                    act.wait_ge(S[f"lg_turned{l}"], 2 * b + (h + 1))
                    hi(lth[l][:, 2 * h:2 * h + 2], ps[:, T_BANK[l] + h, :], 1.0, S[f"lg_xh{l}"])

            def normalise(dst, base, cols, done):
                act.sem_inc(S["act_turn"], 1)
                for j in range(TB):
                    k = cols + j
                    last = a.activation(dst[:, j, 0:D], X[:, ds(base + j * D, D)], ACT.Identity,
                                        bias=shiftn[:, k:k + 1], scale=rstd[:, k:k + 1])
                last.then_inc(done, 1)

            def norm_old(l, n, rows):
                act.wait_ge(S[f"coef{l}_ready"], n + 1)
                if rows is xnr:
                    act.wait_ge(S[f"rows{l}_sent"], 2 * TB * 16 * (n - 1) + 16)
                normalise(rows, (n - 1) * (TB * D), 0, S[f"lg_norm{l}"])

            def norm_next(l, n):
                normalise(xn, (n + 1) * (TB * D), TB, S[f"norm{l}_ready"])

            def norm_first(l):
                act.wait_ge(S[f"coef{l}_ready"], 1)
                normalise(xn, 0, 0, S[f"norm{l}_ready"])

            act.wait_ge(S["prep0_in"], 160)
            a.activation(tg[:], gates_sb[:], ACT.Tanh).then_inc(S["tanh_ready"], 1)

            def attention0(n, old, new, following, weights):
                if new:
                    for h in range(2):
                        act.wait_ge(S["turned0"], 2 * n + (h + 1))
                        hi(xth[:, 2 * h:2 * h + 2], ps[:, h, :], 1.0, S["xh0"])
                    if weights:
                        split_weights(0, n, 0)
                        split_weights(0, n, 1)
                    act.wait_ge(S["score0_shifted"], n + 1)
                    a.activation(sm, sm, ACT.Exp, scale=1.0 / (XS * WS)).then_inc(S["exp0_ready"], 1)
                if old:
                    norm_old(0, n, xnr if new else xnr_last)
                if new:
                    act.wait_ge(S["prob0_turned"], n + 1)
                    hi(pth, ps[:, 3, :], PS, S["ph0"])
                if old:
                    logits_turn(0, n - 1)
                if following:
                    norm_next(0, n)
            norm_first(0)
            attention0(0, False, True, True, True)
            with act.Fori(1, NB - 1) as n:
                attention0(n, True, True, True, True)
            attention0(NB - 1, True, True, False, False)
            attention0(NB, True, False, False, False)
            for h in range(2):
                split_weights(0, E - 1, h)

            def gate_weights(l):
                act.wait_ge(S[f"diff{l}_ready"], 1)
                a.activation(dif[:], dif[:], ACT.Exp, scale=1.0 / (XS * WS)).then_inc(S[f"e2{l}_ready"], 1)
            gate_weights(0)

            def experts(l):
                f = F[l]

                def xhi(t):
                    act.wait_ge(f["turned"], t + 1)
                    hi(fxh, ps[:, 0, 0:D], 1.0, f["xh"])

                def gate(t, first):
                    if l == 0:
                        for h in range(2):
                            act.wait_ge(f["h_ready"], 2 * t + (h + 1))
                            if not first:
                                act.wait_ge(f["g_turned"], 2 * t + (h - 1))
                            a.activation(g32[:, h * 512:(h + 1) * 512], ps[:, 1 + h, :], ACT.Gelu,
                                         scale=1.0 / (XS * WS)).then_inc(f["act_done"], 1)
                    else:
                        act.wait_ge(f["h_ready"], 2 * t + 1)
                        if not first:
                            act.wait_ge(f["g_ready"], t)
                        a.activation(s32, ps[:, 1, :], ACT.Silu, scale=1.0 / (XS * WS)).then_inc(f["act_done"], 1)

                def ghi(t, first):
                    for h in range(2 - l):
                        act.wait_ge(f["g_turned"], (2 - l) * t + (h + 1))
                        if not first:
                            act.wait_ge(f["y_ready"], t)
                        hi(fgh[:, h * 512:(h + 1) * 512], ps[:, 3 + h, :], HS, f["gh"])
                xhi(0)
                gate(0, True)
                xhi(1)
                ghi(0, True)
                with act.Fori(1, FT - 1) as t:
                    gate(t, False)
                    xhi(t + 1)
                    ghi(t, False)
                gate(FT - 1, False)
                ghi(FT - 1, False)
            experts(0)

            def attention1(n, old, new, following):
                if new:
                    for h in range(2):
                        act.wait_ge(S["turned1"], 2 * n + (h + 1))
                        hi(xth[:, 2 * h:2 * h + 2], ps[:, h, :], 1.0, S["xh1"])
                    for c in range(DC):
                        act.wait_ge(S["q1_ready"], 2 * n + (c + 1))
                        if c:
                            act.wait_ge(S["q1_evac"], 2 * n + 1)
                        a.activation(qh[:, c, :], ps[:, S_BANK[0] + c, :], ACT.Identity, bias=ba1[:, 1, c:c + 1],
                                     scale=WS / 4 / (XS * WS))
                        a.activation(q32, ps[:, S_BANK[0] + c, :], ACT.Identity, bias=ba1[:, 1, c:c + 1],
                                     scale=WS / 4 / (XS * WS)).then_inc(S["qh1"], 1)
                    split_weights(1, n, 0)
                if old:
                    norm_old(1, n, xnr if new else xnr_last)
                if not new:
                    logits_turn(1, n - 1)
                    return
                for j in range(TB):
                    act.wait_ge(S["score1_shifted"], TB * n + (j + 1))
                    a.activation(es, es, ACT.Exp, scale=1.0 / (WS * WS)).then_inc(S["exp1_ready"], 1)
                    if j == 0 and old:
                        logits_turn(1, n - 1)
                    if j == TB - 1:
                        split_weights(1, n, 1)
                    for h in range(2):
                        act.wait_ge(S["exp1_turned"], 2 * TB * n + (2 * j + h + 1))
                        hi(eth[:, 4 * h:4 * h + 4, :], ps[:, 6 + h, :], PS, S["eh1"])
                    if j >= 2:
                        act.wait_ge(S["ctx1_turned"], 2 * n + (j - 1))
                        hi(xth[:, 2 * (j - 2):2 * (j - 2) + 2], ps[:, S_BANK[0] + j - 2, :], WS, S["ch1"])
                if following:
                    norm_next(1, n)
            norm_first(1)
            attention1(0, False, True, True)
            with act.Fori(1, NB - 1) as n:
                attention1(n, True, True, True)
            attention1(NB - 1, True, True, False)
            attention1(NB, True, False, False)
            gate_weights(1)
            experts(1)

        @block.vector
        def _(dve):
            v = nc.vector
            own = Done(dve, S["dve_order"])

            def norm_stats(base, cols):
                dve.sem_inc(S["dve_turn"], 1)
                for j in range(TB):
                    own.add(v.bn_stats(stats[:, cols + j, :], X[:, ds(base + j * D, D)]))

            def advance(steps, n=1):
                for _ in range(n):
                    next(steps, None)

            def norm_coef(n, done, others=None):
                others = others or iter(())
                st, mn, rs, l_, va = stats[:, 0:n], mean[:, 0:n], rstd[:, 0:n], lt[:, 0:n], ve[:, 0:n]
                own.wait()
                own.add(v.tensor_tensor(mn, st[:, :, 1], st[:, :, 4], ALU.add))
                own.add(v.tensor_tensor(l_, st[:, :, 1], st[:, :, 4], ALU.subtract))
                own.add(v.tensor_tensor(va, st[:, :, 2], st[:, :, 5], ALU.add))
                advance(others)
                own.wait()
                own.add(v.scalar_tensor_tensor(out=l_, in0=l_, scalar=0.25, in1=l_, op0=ALU.mult, op1=ALU.mult))
                advance(others)
                own.wait()
                own.add(v.scalar_tensor_tensor(out=va, in0=va, scalar=1.0 / D, in1=l_, op0=ALU.mult, op1=ALU.add))
                advance(others)
                own.wait()
                own.add(v.tensor_scalar(va, va, EPS, 1.0 / XS / XS, ALU.add, ALU.mult))
                advance(others)
                own.wait()
                own.add(v.tensor_scalar(rs.bitcast(I32), va.bitcast(I32), 1, None, ALU.logical_shift_right))
                advance(others)
                own.wait()
                own.add(v.tensor_scalar(rs.bitcast(I32), rs.bitcast(I32), -1.0, RSQRT_SEED, ALU.mult, ALU.add))
                advance(others)
                own.wait()
                for _ in range(3):
                    own.add(v.tensor_tensor(l_, rs, rs, ALU.mult))
                    advance(others)
                    own.wait()
                    own.add(v.scalar_tensor_tensor(out=l_, in0=l_, scalar=-0.5, in1=va, op0=ALU.mult, op1=ALU.mult))
                    advance(others)
                    own.wait()
                    own.add(v.scalar_tensor_tensor(out=rs, in0=l_, scalar=1.5, in1=rs, op0=ALU.add, op1=ALU.mult))
                    advance(others)
                    own.wait()
                v.scalar_tensor_tensor(out=shiftn[:, 0:n], in0=mn, scalar=-0.5, in1=rs, op0=ALU.mult, op1=ALU.mult).then_inc(done, 1)
                advance(others, 99)

            def norm_first(l):
                norm_stats(0, 0)
                norm_stats(TB * D, TB)
                norm_coef(2 * TB, S[f"coef{l}_ready"])

            def lo(dst, src, scale, hi_part, done):
                v.scalar_tensor_tensor(out=dst, in0=src, scalar=scale, in1=hi_part, op0=ALU.mult, op1=ALU.subtract).then_inc(done, 1)

            def split_third(l, e, h, i):
                if i == 0:
                    dve.wait_ge(w_hi[l], 2 * e + (h + 1))
                    dve.sem_inc(S["dve_turn"], 1)
                n = HALF[l] // 3
                at = h * HALF[l] + i * n
                ins = v.scalar_tensor_tensor(out=wlo(l, e, at, n), in0=stage[:, h, i * n:(i + 1) * n], scalar=WS, in1=whi(l, e, at, n),
                                             op0=ALU.mult, op1=ALU.subtract)
                if i == 2:
                    ins.then_inc(w_lo[l], 1)

            def split_weights(l, e, h):
                dve.wait_ge(w_hi[l], 2 * e + (h + 1))
                lo(wlo(l, e, h * HALF[l], HALF[l]), stage[:, h, 0:HALF[l]], WS, whi(l, e, h * HALF[l], HALF[l]), w_lo[l])

            dve.wait_ge(S["consts_ready"], 1)
            dve.wait_ge(S["prep0_in"], 160)
            dve.wait_ge(S["tanh_ready"], 1)
            own.add(v.tensor_copy(fill[:], region0[:]))
            own.add(v.tensor_scalar(tgs[:, 0:1], tg[:, 0:1], 1.0 / (XS * WS), None, ALU.mult))
            own.add(v.tensor_scalar(tgs[:, 1:2], tg[:, 2:3], 1.0 / (WS * WS), None, ALU.mult))
            own.add(v.memset(smw[:, :, KEYS:P], 0.0))
            own.add(v.memset(vwh[KEYS:P], 0.0))
            own.add(v.memset(vwl[KEYS:P], 0.0))
            for half, dst in ((0, kt0), (1, vt0)):
                dve.wait_ge(S["k0v0_ready"], half + 1)
                for c in range(DC):
                    last = v.tensor_scalar(dst[:, c, :], ps[:, 2 * half + c, :], ba0[:, half, c:c + 1], None, ALU.add)
                last.then_inc(S["k0_copied"], 1)

            def split_ps(h, l_, src, scale):
                own.add(v.tensor_scalar(h, src, scale, None, ALU.mult))
                own.wait()
                own.add(v.scalar_tensor_tensor(out=l_, in0=src, scalar=scale, in1=h, op0=ALU.mult, op1=ALU.subtract))
            split_ps(wo0h, wo0l, wa0[3], WS)
            split_ps(rth[:], rtl[:], rts[:, 0], WS)
            dve.wait_ge(S["x_in0"], 16)
            norm_first(0)
            dve.wait_ge(S["g0_ready"], 1)
            for c in range(DC):
                split_ps(gh[:, c, :], gl[:, c, :], ps[:, 4 + c, :], WS / D ** 0.5)
            split_ps(cbh, cbl, ps[0:1, 6, :], WS / D ** 0.5)
            own.wait()
            dve.sem_inc(S["g0_copied"], 1)
            for q in range(4):
                dve.wait_ge(S["vw0_ready"], q + 1)
                split_ps(vwh[0:KEYS, 2 * q:2 * q + 2, :], vwl[0:KEYS, 2 * q:2 * q + 2, :],
                         ps[0:KEYS, q, :].rearrange("p (a b) -> p a b", a=2), WS)
            own.wait()
            dve.sem_inc(S["w0_split"], 1)
            dve.wait_ge(S["x_in"], 16)

            def residual(l, b, gate_col):
                for h in range(2):
                    dve.wait_ge(S[f"attn{l}_ready"], 2 * b + (h + 1))
                    dve.sem_inc(S["dve_turn"], 1)
                    for i in range(2):
                        at = X[:, ds(b * (TB * D) + (2 * h + i) * D, D)]
                        own.add(v.scalar_tensor_tensor(out=at, in0=ps[:, O_BANK[l] + h, i * D:(i + 1) * D], scalar=tgs[:, gate_col:gate_col + 1],
                                                       in1=at, op0=ALU.mult, op1=ALU.add))
                own.wait()

            def logits_lo(l, b):
                for h in range(2):
                    dve.wait_ge(S[f"lg_xh{l}"], 2 * b + (h + 1))
                    lo(ltl[l][:, 2 * h:2 * h + 2], ps[:, T_BANK[l] + h, :], 1.0, lth[l][:, 2 * h:2 * h + 2], S[f"lg_xl{l}"])

            def take_logits(l, b):
                dve.wait_ge(S[f"logits{l}_ready"], b + 1)
                bank = LOGITS_BANK[l]
                own.add(v.tensor_copy(logit[:], ps[:, bank, 0:TB * E].rearrange("p (a b) -> p a b", a=TB)))

            def choose(l, b, rows):
                own.wait()
                for k, m in ((0, m1), (1, m2)):
                    own.add(v.tensor_reduce(m[:], logit[:], axis=AX, op=ALU.max))
                    yield
                    own.wait()
                    own.add(v.tensor_tensor(eq[:], logit[:], spread(m[:], 2, (P, TB, E)), ALU.is_equal))
                    yield
                    own.wait()
                    own.add(v.tensor_tensor(eq[:], eq[:], revidx[:], ALU.mult))
                    yield
                    own.wait()
                    own.add(v.tensor_reduce(mi[:, k, :], eq[:], axis=AX, op=ALU.max))
                    yield
                    own.wait()
                    own.add(v.tensor_tensor(oh[:, k], eq[:], spread(mi[:, k, :], 2, (P, TB, E)), ALU.is_equal))
                    yield
                    own.wait()
                    if k == 0:
                        own.add(v.scalar_tensor_tensor(out=logit[:], in0=oh[:, 0], scalar=FAR, in1=logit[:], op0=ALU.mult, op1=ALU.add))
                        yield
                        own.wait()
                v.tensor_tensor(sel[:], oh[:, 0], oh[:, 1], ALU.add).then_inc(S[f"sel{l}_ready"], 1)
                own.add(v.tensor_tensor(dif[:, ds(b * TB, TB)], m2[:], m1[:], ALU.subtract))
                own.add(v.tensor_scalar(rows[:, :, D:D + 1], tokid[:, ds(b * TB, TB)].unsqueeze(2), 0.0, None, ALU.add))
                own.add(v.tensor_copy(rows[:, :, D + 1:D + 2], mi[:, 0, :].unsqueeze(2)))

            def place(l, b, index):
                dve.wait_ge(S[f"count{l}_ready"], b + 1)
                bank = COUNTS_BANK[l]
                own.add(v.tensor_tensor(posr[:], ps[:, bank, 0:TB * E].rearrange("p (a b) -> p a b", a=TB),
                                        spread(fill[:], 1, (P, TB, E)), ALU.add))
                own.wait()
                own.add(v.tensor_tensor(fill[:], ps[:, bank, TB * E:(TB + 1) * E], fill[:], ALU.add))
                own.add(v.tensor_tensor(pk[:], oh[:], spread(posr[:], 1, (P, 2, TB, E)), ALU.mult))
                own.wait()
                dve.sem_inc(S[f"count{l}_taken"], 1)
                own.add(v.tensor_reduce(slot[:], pk[:].rearrange("p k t e -> p (k t) e"), axis=AX, op=ALU.add))
                own.wait()
                v.tensor_copy(index[:], slot[:]).then_inc(S[f"slots{l}_ready"], 1)

            def attention0(n, old, new, following, weights):
                if old:
                    residual(0, n - 1, 0)
                if new:
                    for h in range(2):
                        dve.wait_ge(S["xh0"], 2 * n + (h + 1))
                        lo(xtl[:, 2 * h:2 * h + 2], ps[:, h, :], 1.0, xth[:, 2 * h:2 * h + 2], S["xl0"])
                if old:
                    norm_stats((n - 1) * (TB * D), 0)
                    if following:
                        norm_stats((n + 1) * (TB * D), TB)
                if new:
                    dve.wait_ge(S["score0_ready"], n + 1)
                    scores = ps[:, 2, 0:TB * KEYS].rearrange("p (a b) -> p a b", a=TB)
                    own.add(v.tensor_reduce(m1[:], scores, axis=AX, op=ALU.max))
                    own.wait()
                    v.tensor_tensor(sm, scores, spread(m1[:], 2, (P, TB, KEYS)), ALU.subtract).then_inc(S["score0_shifted"], 1)
                if old:
                    norm_coef(2 * TB if following else TB, S["coef0_ready"])
                if new:
                    dve.wait_ge(S["exp0_ready"], n + 1)
                    own.add(v.tensor_reduce(m1[:], sm, axis=AX, op=ALU.add))
                    own.wait()
                    own.add(v.reciprocal(m2[:], m1[:]))
                    own.wait()
                    v.tensor_tensor(sm, sm, spread(m2[:], 2, (P, TB, KEYS)), ALU.mult).then_inc(S["prob0_ready"], 1)
                    if weights:
                        split_weights(0, n, 0)
                    dve.wait_ge(S["ph0"], n + 1)
                    lo(ptl, ps[:, 3, :].rearrange("p (a b) -> p a b", a=TB), PS, pth, S["pl0"])
                if old:
                    logits_lo(0, n - 1)
                if weights:
                    split_weights(0, n, 1)
                if old:
                    take_logits(0, n - 1)
                    advance(choose(0, n - 1, xnr if new else xnr_last), 99)
                    place(0, n - 1, sloti if new else sloti_last)

            def repeat(first, end, per, body):
                start = own.base + own.n
                with dve.Fori(first, end) as n:
                    own.base, own.n = (n - first) * per + start, 0
                    body(n)
                    assert own.n == per, (own.n, per)
                own.base, own.n = start + (end - first) * per, 0
            attention0(0, False, True, True, True)
            repeat(1, NB - 1, STEPS0, lambda n: attention0(n, True, True, True, True))
            attention0(NB - 1, True, True, False, False)
            attention0(NB, True, False, False, False)
            own.wait()

            def table(l):
                own.wait()
                dve.sem_inc(S[f"diff{l}_ready"], 1)
                own.add(v.tensor_copy(fill_end[:], fill[:]))
                own.wait()
                dve.sem_inc(S[f"fill{l}_ready"], 1)
                own.add(v.tensor_tensor(endA[:], fill[:], region0[:], ALU.subtract))
                own.wait()
                own.add(v.tensor_tensor(over, spread(endA[:], 2, (P, E, NT)), steps128[:], ALU.is_gt))
                own.wait()
                own.add(v.tensor_reduce(tiles[:], over, axis=AX, op=ALU.add))
                own.wait()
                own.add(v.tensor_copy(endA[:], tiles[:]))
                own.wait()
                src, dst = endA, endB
                for step in (1, 2, 4):
                    own.add(v.tensor_copy(dst[:, 0:step], src[:, 0:step]))
                    own.add(v.tensor_tensor(dst[:, step:E], src[:, step:E], src[:, 0:E - step], ALU.add))
                    own.wait()
                    src, dst = dst, src
                own.add(v.tensor_tensor(ended, spread(src[:], 1, (P, FT, E)), spread(tileno[:], 2, (P, FT, E)), ALU.is_le))
                own.wait()
                own.add(v.tensor_tensor(skipped, ended, spread(tiles[:], 1, (P, FT, E)), ALU.mult))
                own.add(v.tensor_reduce(nended, ended, axis=AX, op=ALU.add))
                own.wait()
                own.add(v.tensor_reduce(tskip, skipped, axis=AX, op=ALU.add))
                own.add(v.tensor_scalar(code[:], nended, -1.0, float(E), ALU.mult, ALU.add))
                own.add(v.tensor_scalar(expert[:], nended, float(E - 1), None, ALU.min))
                own.wait()
                own.add(v.tensor_tensor(tskip, tileno[:], tskip, ALU.subtract))
                own.add(v.tensor_scalar(nended, nended, float(REGION), None, ALU.mult))
                own.wait()
                own.add(v.scalar_tensor_tensor(out=tskip, in0=tskip, scalar=float(P), in1=nended, op0=ALU.mult, op1=ALU.add))
                own.wait()
                own.add(v.tensor_scalar(rowbase[:], tskip, float(E * REGION), None, ALU.min))
                own.wait()
                dve.sem_inc(S[f"table{l}_ready"], 1)
                own.add(v.tensor_copy(packing[:], expert[:, UNROLL:UNROLL * TURNS + 1:UNROLL]))
                own.wait()
                for i in reversed(range(UNROLL)):
                    own.add(v.scalar_tensor_tensor(out=packing[:], in0=packing[:], scalar=16.0,
                                                   in1=expert[:, i:i + UNROLL * (TURNS - 1) + 1:UNROLL], op0=ALU.mult, op1=ALU.add))
                    own.wait()
                own.add(v.tensor_copy(packed[:], packing[:]))
                own.wait()
                dve.sem_inc(S[f"packed{l}_ready"], 1)
                dve.wait_ge(S[f"e2{l}_ready"], 1)
                own.add(v.tensor_scalar(wgt[:, 0, :], dif[:], 1.0, None, ALU.add))
                own.wait()
                own.add(v.reciprocal(wgt[:, 0, :], wgt[:, 0, :]))
                own.wait()
                own.add(v.tensor_scalar(wgt[:, 0, :], wgt[:, 0, :], tg[:, 2 * l + 1:2 * l + 2], None, ALU.mult))
                own.wait()
                own.add(v.tensor_tensor(wgt[:, 1, :], wgt[:, 0, :], dif[:], ALU.mult))
                own.wait()

            def experts(l):
                f = F[l]
                dve.sem_inc(f["y_out"], 1)

                def xlo(t):
                    dve.wait_ge(f["xh"], t + 1)
                    lo(fxl, ps[:, 0, 0:D].rearrange("p (a b) -> p a b", a=DC), 1.0, fxh, f["xl"])

                def ids(t, part, slot, half):
                    parity = slot % 2
                    dve.wait_ge(f[f"row_in{slot}"], 16 * part + 16)
                    dve.wait_ge(f[f"sent{parity}"], 16 * half + 16)
                    dve.sem_inc(S["dve_turn"], 1)
                    own.add(v.tensor_tensor(idt[:, 0:1], row_in[:, slot, D + 1:D + 2], code[:, ds(t, 1)], ALU.not_equal))
                    own.wait()
                    v.scalar_tensor_tensor(out=idc[:, parity:parity + 1], in0=idt[:, 0:1], scalar=float(TOKENS),
                                           in1=row_in[:, slot, D:D + 1], op0=ALU.mult, op1=ALU.add).then_inc(f["ids"], 1)

                def product(t, first):
                    if l:
                        dve.wait_ge(f["h_ready"], 2 * t + 2)
                        dve.wait_ge(f["act_done"], t + 1)
                        if not first:
                            dve.wait_ge(f["g_turned"], t)
                        v.scalar_tensor_tensor(out=g32[:, 0:512], in0=ps[:, 2, :], scalar=1.0 / (XS * WS), in1=s32,
                                               op0=ALU.mult, op1=ALU.mult).then_inc(f["g_ready"], 1)

                def result(t, parity):
                    dve.wait_ge(f["y_ready"], t + 1)
                    v.tensor_scalar(y32[:, parity, :], ps[:, 5, 0:D], 1.0 / (HS * WS), None, ALU.mult).then_inc(f["y_out"], 1)

                def glo(t):
                    for h in range(2 - l):
                        dve.wait_ge(f["gh"], (2 - l) * t + (h + 1))
                        lo(fgl[:, h * 512:(h + 1) * 512], ps[:, 3 + h, :], HS, fgh[:, h * 512:(h + 1) * 512], f["gl"])

                def turn(t, part, slot, half):
                    product(t, False)
                    xlo(t + 1)
                    result(t - 1, 1 - slot % 2)
                    ids(t, part, slot, half)
                    glo(t)
                xlo(0)
                product(0, True)
                xlo(1)
                ids(0, 0, 0, 0)
                glo(0)
                start = own.base + own.n
                with dve.Fori(0, TURNS) as m:
                    own.base, own.n = UNROLL * m + start, 0
                    for i in range(1, UNROLL + 1):
                        turn(UNROLL * m + i, m + i // SLOTS, i % SLOTS, UNROLL // 2 * m + i // 2)
                own.base, own.n = start + UNROLL * TURNS, 0
                for t in range(1 + UNROLL * TURNS, FT - 1):
                    turn(t, t // SLOTS, t % SLOTS, t // 2)
                t = FT - 1
                product(t, False)
                result(t - 1, 1 - t % 2)
                ids(t, t // SLOTS, t % SLOTS, t // 2)
                glo(t)
                result(t, t % 2)

            def combine_batch(b):
                dve.wait_ge(back_in[0][b % 4], 32 * (b // 4) + 32)
                for k in range(2):
                    for j in range(TB):
                        at = tok(b * TB + j)
                        own.add(v.scalar_tensor_tensor(out=at, in0=back[b % 4][k][:, j, :], scalar=wgt[:, k, b * TB + j:b * TB + j + 1],
                                                       in1=at, op0=ALU.mult, op1=ALU.add))
                    own.wait()
                dve.sem_inc(back_used[0], 1)

            def combine(l, done):
                dve.sem_inc(back_used[l], 4)
                start = own.base + own.n
                with dve.Fori(0, NB // 4) as m:
                    own.base, own.n = m * (4 * 2 * TB) + start, 0
                    for r in range(4):
                        dve.wait_ge(back_in[l][r], 32 * m + 32)
                        dve.sem_inc(S["dve_turn"], 1)
                        for k in range(2):
                            for j in range(TB):
                                at = X[:, ds(m * (4 * TB * D) + (r * TB + j) * D, D)]
                                own.add(v.scalar_tensor_tensor(out=at, in0=back[r][k][:, j, :],
                                                               scalar=wgt[:, k, ds(m * (4 * TB) + (r * TB + j), 1)],
                                                               in1=at, op0=ALU.mult, op1=ALU.add))
                            own.wait()
                        dve.sem_inc(back_used[l], 1)
                        if done:
                            dve.sem_inc(done, 1)
                own.base, own.n = start + NB * 2 * TB, 0

            table(0)
            for h in range(2):
                split_weights(0, E - 1, h)
            experts(0)
            dve.sem_inc(back_used[0], 4)
            dve.wait_ge(S["prep1_in"], 16 * 8)
            split_ps(wq1h, wq1l, wq1, WS)
            split_ps(wo1h, wo1l, wo1, WS)
            split_ps(bo1h, bo1l, bo1s, WS * WS / XS)
            split_ps(rth[:], rtl[:], rts[:, 1], WS)
            own.add(v.tensor_scalar(ba1[:, 1, :], ba1[:, 1, :], WS / 4, None, ALU.mult))
            own.add(v.tensor_copy(fill[:], region0[:]))
            own.add(v.memset(vbl[:, :, 32:34], 0.0))
            own.add(v.tensor_scalar(vbh[:, :, 32:34], spread(smask[:], 1, (P, PAIRS, 2)), WS, None, ALU.mult))
            for c in range(DC):
                dve.wait_ge(S["kv1_ready"], c + 1)
                own.add(v.tensor_scalar(q32, ps[:, 2 + c, :], ba1[:, 0, c:c + 1], None, ALU.add))
                own.wait()
                split_ps(kt1h[:, c, :], kt1l[:, c, :], q32, WS)
                own.wait()
            dve.sem_inc(S["w1_split"], 1)
            combine_batch(0)
            combine_batch(1)
            norm_first(1)
            for q in range(4):
                dve.wait_ge(S["kv1_ready"], DC + q + 1)
                v.tensor_copy(v1[:, 2 * q:2 * q + 2, :], ps[:, 4 + q, :].rearrange("p (a b) -> p a b", a=2)).then_inc(S["kv1_copied"], 1)
            dve.wait_ge(S["kv1_copied"], 4)
            combine_batch(2)

            def attention1(n, old, new, following):
                if old:
                    residual(1, n - 1, 1)
                if new:
                    for h in range(2):
                        dve.wait_ge(S["xh1"], 2 * n + (h + 1))
                        lo(xtl[:, 2 * h:2 * h + 2], ps[:, h, :], 1.0, xth[:, 2 * h:2 * h + 2], S["xl1"])
                if old:
                    norm_stats((n - 1) * (TB * D), 0)
                    if following:
                        norm_stats((n + 1) * (TB * D), TB)
                if not old:
                    combine_batch(3)
                if not new:
                    norm_coef(TB, S["coef1_ready"])
                    logits_lo(1, n - 1)
                    take_logits(1, n - 1)
                    advance(choose(1, n - 1, xnr_last), 99)
                    place(1, n - 1, sloti_last)
                    return

                def queries_lo(c):
                    dve.wait_ge(S["qh1"], 2 * n + (c + 1))
                    v.tensor_tensor(ql[:, c, :], q32, qh[:, c, :], ALU.subtract).then_inc(S["q1_evac"], 1)

                def keys(c, dst, src):
                    v.tensor_tensor(dst[:, c, :].rearrange("p (h k) -> p h k", h=HPC),
                                    spread(src[:, c, ds(n * KEYS, KEYS)], 1, (P, HPC, KEYS)),
                                    spread(hmask[:], 2, (P, HPC, KEYS)), ALU.mult).then_inc(S["kb1_ready"], 1)

                def keys_and_values():
                    for c in range(DC):
                        keys(c, kbh, kt1h)
                        yield
                        keys(c, kbl, kt1l)
                        yield
                    own.add(v.tensor_tensor(vb32.rearrange("p a (s f) -> p a s f", s=2),
                                            v1[:, ds(n, 1), :].rearrange("p o (a s f) -> p (o a) s f", a=PAIRS, s=2),
                                            smask[:].unsqueeze(1).unsqueeze(3).broadcast_to((P, PAIRS, 2, HD)), ALU.mult))
                    yield
                    own.wait()
                    own.add(v.tensor_scalar(vbh[:, :, 0:32], vb32, WS, None, ALU.mult))
                    yield
                    own.wait()
                    v.scalar_tensor_tensor(out=vbl[:, :, 0:32], in0=vb32, scalar=WS, in1=vbh[:, :, 0:32],
                                           op0=ALU.mult, op1=ALU.subtract).then_inc(S["kb1_ready"], 1)
                dve.sem_inc(S["dve_turn"], 1)
                operands = keys_and_values()
                if old:
                    queries_lo(0)
                    advance(operands, 2)
                    queries_lo(1)
                    norm_coef(2 * TB if following else TB, S["coef1_ready"], operands)
                else:
                    queries_lo(0)
                    advance(operands, 99)
                    queries_lo(1)
                    combine_batch(4)

                def largest(j):
                    dve.wait_ge(S["score1_ready"], TB * n + (j + 1))
                    scores = ps[:, S_BANK[j % 2]:S_BANK[j % 2] + 2, :].rearrange("p a (h k) -> p (a h) k", k=KEYS)
                    own.add(v.tensor_reduce(m16[:, j % 2], scores, axis=AX, op=ALU.max))
                    return scores

                def shift(j, scores):
                    own.wait()
                    if j:
                        dve.wait_ge(S["exp1_turned"], 2 * TB * n + 2 * j)
                    v.tensor_tensor(es.rearrange("p (h k) -> p h k", k=KEYS), scores, spread(m16[:, j % 2], 2, (P, HEADS, KEYS)),
                                    ALU.subtract).then_inc(S["score1_shifted"], 1)

                def elo(j, h):
                    dve.wait_ge(S["eh1"], 2 * TB * n + (2 * j + h + 1))
                    lo(etl[:, 4 * h:4 * h + 4, :], ps[:, 6 + h, :].rearrange("p (a b) -> p a b", a=4), PS,
                       eth[:, 4 * h:4 * h + 4, :], S["el1"])

                def context(j):
                    dve.wait_ge(S["pv1_ready"], TB * n + (j + 1))
                    pv = ps[:, j % 2, 0:PAIRS * 34].rearrange("p (a c) -> p a c", c=34)
                    own.add(v.reciprocal(r16[:], pv[:, :, 32:34]))
                    own.wait()
                    v.tensor_tensor(xn[:, j, :].rearrange("p (a s f) -> p a s f", a=PAIRS, s=2),
                                    pv[:, :, 0:32].rearrange("p a (s f) -> p a s f", s=2),
                                    spread(r16[:], 3, (P, PAIRS, 2, HD)), ALU.mult).then_inc(S["ctx1_ready"], 1)
                def context_lo(h):
                    dve.wait_ge(S["ch1"], 2 * n + (h + 1))
                    lo(xtl[:, 2 * h:2 * h + 2], ps[:, S_BANK[0] + h, :], WS, xth[:, 2 * h:2 * h + 2], S["cl1"])
                choice = choose(1, n - 1, xnr) if old else iter(())
                shift(0, largest(0))
                scores = largest(1)
                if old:
                    logits_lo(1, n - 1)
                split_weights(1, n, 0)
                if not old:
                    combine_batch(5)
                if old:
                    take_logits(1, n - 1)
                shift(1, scores)
                for j in range(TB):
                    if j >= 1 and j + 1 < TB:
                        scores = largest(j + 1)
                        advance(choice, 2)
                    if j:
                        context(j - 1)
                        advance(choice, 2)
                    if old and j == 2:
                        place(1, n - 1, sloti)
                    if not old and j in (1, 2):
                        combine_batch(5 + j)
                    if j >= 1 and j + 1 < TB:
                        shift(j + 1, scores)
                        advance(choice, 2)
                    if j == TB - 1:
                        split_third(1, n, 1, 0)
                    for h in range(2):
                        elo(j, h)
                        advance(choice, 2 if j == 0 else 99)
                    if j == 2:
                        context_lo(0)
                split_third(1, n, 1, 1)
                context(TB - 1)
                context_lo(1)
                split_third(1, n, 1, 2)
            attention1(0, False, True, True)
            repeat(1, NB - 1, STEPS1, lambda n: attention1(n, True, True, True))
            attention1(NB - 1, True, True, False)
            attention1(NB, True, False, False)
            table(1)
            experts(1)
            combine(1, S["out_ready"])

        @block.tensor
        def _(pe):
            mm = nc.tensor.matmul

            def turn4(src, done, bank=0):
                for j in range(TB):
                    for c in range(DC):
                        at = (j % 2) * D + c * P
                        last = nc.tensor.transpose(ps[:, bank + j // 2, at:at + P], src[:, j, c * P:(c + 1) * P], ident[:])
                    if j % 2:
                        last.then_inc(done, 1)

            def passes(dst, left, right, start=True, stop=True):
                n = len(left)
                for i in range(n):
                    for q, (a_, b_) in enumerate(rh_rl):
                        last = mm(dst, left[i][a_], right[i][b_], start=start and i == 0 and q == 0,
                                  stop=stop and i == n - 1 and q == 2)
                return last

            def turn_rows(l, b, rows):
                pe.wait_ge(S[f"lg_norm{l}"], b + 1)
                turn4(rows, S[f"lg_turned{l}"], T_BANK[l])

            def logits(l, b):
                bank = LOGITS_BANK[l]
                for h in range(2):
                    pe.wait_ge(S[f"lg_xl{l}"], 2 * b + (h + 1))
                    for j in (2 * h, 2 * h + 1):
                        last = passes(ps[:, bank, j * E:(j + 1) * E], [(lth[l][:, j, c, :], ltl[l][:, j, c, :]) for c in range(DC)],
                                      [(rth[:, c, :], rtl[:, c, :]) for c in range(DC)])
                last.then_inc(S[f"logits{l}_ready"], 1)

            def counts(l, b):
                pe.wait_ge(S[f"sel{l}_ready"], b + 1)
                bank = COUNTS_BANK[l]
                s2 = sel[:].rearrange("p a b -> p (a b)")
                mm(ps[:, bank, 0:TB * E], before[:], s2, start=True, stop=False)
                for j in range(1, TB):
                    mm(ps[:, bank, j * E:TB * E], ones16[:], s2[:, 0:(TB - j) * E], start=False, stop=False)
                for j in range(TB):
                    last = mm(ps[:, bank, TB * E:(TB + 1) * E], ones16[:], s2[:, j * E:(j + 1) * E], start=False, stop=j == TB - 1)
                last.then_inc(S[f"count{l}_ready"], 1)

            pe.wait_ge(S["consts_ready"], 1)
            pe.wait_ge(S["prep0_in"], 160)
            for half in range(2):
                for c in range(DC):
                    for k in range(DC):
                        last = mm(ps[:, 2 * half + c, :], wa0[half][:, k, c * P:(c + 1) * P], ctx0[:, k, :], start=k == 0, stop=k == DC - 1)
                last.then_inc(S["k0v0_ready"], 1)
            pe.wait_ge(S["k0_copied"], 1)
            for c in range(DC):
                for k in range(DC):
                    mm(ps[:, 4 + c, :], wa0[2][:, k, c * P:(c + 1) * P], kt0[:, k, :], start=k == 0, stop=k == DC - 1)
            for k in range(DC):
                last = mm(ps[0:1, 6, :], ba0[:, 2, k:k + 1], kt0[:, k, :], start=k == 0, stop=k == DC - 1)
            last.then_inc(S["g0_ready"], 1)
            pe.wait_ge(S["k0_copied"], 2)
            for b in range(NB):
                dst = ps[:, b // 2, (b % 2) * D:(b % 2 + 1) * D]
                for k in range(DC):
                    mm(dst[0:KEYS, :], vt0[:, k, b * KEYS:(b + 1) * KEYS], wa0[3][:, k, :], start=k == 0, stop=False)
                last = mm(dst[0:KEYS, :], onesf[:, 0:KEYS], bo0s, start=False, stop=True)
                if b % 2:
                    last.then_inc(S["vw0_ready"], 1)
            pe.wait_ge(S["w0_split"], 1)

            def turn_new(l, n):
                pe.wait_ge(S[f"norm{l}_ready"], n + 1)
                turn4(xn, S[f"turned{l}"])

            def attention0(n, old, new, following):
                if new:
                    for j in range(TB):
                        if j % 2 == 0:
                            pe.wait_ge(S["xl0"], 2 * n + (j // 2 + 1))
                        dst = ps[:, 2, j * KEYS:(j + 1) * KEYS]
                        passes(dst, [(xth[:, j, c, :], xtl[:, j, c, :]) for c in range(DC)],
                               [(gh[:, c, ds(n * KEYS, KEYS)], gl[:, c, ds(n * KEYS, KEYS)]) for c in range(DC)], stop=False)
                        mm(dst, rowscale[:], cbh[:, ds(n * KEYS, KEYS)], start=False, stop=False)
                        last = mm(dst, rowscale[:], cbl[:, ds(n * KEYS, KEYS)], start=False, stop=True)
                    last.then_inc(S["score0_ready"], 1)
                    pe.wait_ge(S["prob0_ready"], n + 1)
                    for j in range(TB):
                        last = nc.tensor.transpose(ps[:, 3, j * P:(j + 1) * P], smw[:, j, :], ident[:])
                    last.then_inc(S["prob0_turned"], 1)
                if old:
                    turn_rows(0, n - 1, xnr if new else xnr_last)
                if new:
                    pe.wait_ge(S["pl0"], n + 1)
                    pe.sem_inc(S["pe_turn"], 1)
                    for j in range(TB):
                        dst = ps[:, O_BANK[0] + j // 2, (j % 2) * D:(j % 2 + 1) * D]
                        passes(dst, [(xth[:, j, c, :], xtl[:, j, c, :]) for c in range(DC)],
                               [(wo0h[:, c, :], wo0l[:, c, :]) for c in range(DC)], stop=False)
                        last = passes(dst, [(pth[:, j, :], ptl[:, j, :])], [(vwh[:, ds(n, 1), :], vwl[:, ds(n, 1), :])], start=False)
                        if j % 2:
                            last.then_inc(S["attn0_ready"], 1)
                        if old and j == 1:
                            logits(0, n - 1)
                    if following:
                        turn_new(0, n + 1)
                else:
                    logits(0, n - 1)
                if old:
                    counts(0, n - 1)
            turn_new(0, 0)
            attention0(0, False, True, True)
            with pe.Fori(1, NB - 1) as n:
                attention0(n, True, True, True)
            attention0(NB - 1, True, True, False)
            attention0(NB, True, False, False)

            def experts(l):
                f = F[l]
                n = 2 - l

                def A(t, part, slot):
                    pe.wait_ge(f[f"row_in{slot}"], 16 * part + 16)
                    for c in range(DC):
                        last = nc.tensor.transpose(ps[:, 0, c * P:(c + 1) * P], row_in[:, slot, c * P:(c + 1) * P], ident[:])
                    last.then_inc(f["turned"], 1)

                def B(t, e, first):
                    pe.wait_ge(f["xl"], t + 1)
                    for h in range(2):
                        if not first:
                            pe.wait_ge(f["act_done"], 2 * t + (h - 1)) if l == 0 else pe.wait_ge(f["g_ready"], t)
                        last = passes(ps[:, 1 + h, :], [(fxh[:, c, :], fxl[:, c, :]) for c in range(DC)],
                                      [(whi(l, e, c * 1024 + h * 512, 512), wlo(l, e, c * 1024 + h * 512, 512)) for c in range(DC)])
                        last.then_inc(f["h_ready"], 1)

                def C(t):
                    for h in range(n):
                        pe.wait_ge(f["act_done"] if l == 0 else f["g_ready"], n * t + (h + 1))
                        for i in range(4):
                            at = h * 512 + i * P
                            last = nc.tensor.transpose(ps[:, 3 + h, i * P:(i + 1) * P], g32[:, at:at + P], ident[:])
                        last.then_inc(f["g_turned"], 1)

                def Dn(t, e):
                    pe.wait_ge(f["gl"], n * t + n)
                    pe.wait_ge(f["y_out"], t + 1)
                    last = passes(ps[:, 5, 0:D], [(fgh[:, k * P:(k + 1) * P], fgl[:, k * P:(k + 1) * P]) for k in range(KD[l])],
                                  [(whi(l, e, 2048 + k * D, D), wlo(l, e, 2048 + k * D, D)) for k in range(KD[l])])
                    last.then_inc(f["y_ready"], 1)

                def number(t):
                    return pe.value_load(expert[0:1, ds(t, 1)], min_val=0, max_val=E - 1)

                def turn(t, part, slot, e, e_before):
                    B(t, e, False)
                    A(t + 1, part + (slot + 1) // SLOTS, (slot + 1) % SLOTS)
                    Dn(t - 1, e_before)
                    C(t)
                pe.wait_ge(S[f"table{l}_ready"], 1)
                pe.wait_ge(w_lo[l], 2 * E)
                A(0, 0, 0)
                B(0, number(0), True)
                A(1, 0, 1)
                C(0)
                pe.wait_ge(S[f"packed{l}_ready"], 1)
                with pe.Fori(0, TURNS) as m:
                    numbers = pe.value_load(packed[0:1, ds(m, 1)], min_val=0, max_val=16 ** (UNROLL + 1) - 1)
                    e = [((numbers >> (4 * i)) & 7).with_bounds(min_val=0, max_val=E - 1) for i in range(UNROLL + 1)]
                    for i in range(UNROLL):
                        turn(UNROLL * m + (i + 1), m + (i + 1) // SLOTS, (i + 1) % SLOTS, e[i + 1], e[i])
                for t in range(1 + UNROLL * TURNS, FT - 1):
                    turn(t, t // SLOTS, t % SLOTS, number(t), number(t - 1))
                t = FT - 1
                B(t, number(t), False)
                Dn(t - 1, number(t - 1))
                C(t)
                Dn(t, number(t))
            experts(0)

            pe.wait_ge(S["prep1_in"], 16 * 8)
            for c in range(DC):
                for k in range(DC):
                    last = mm(ps[:, 2 + c, :], wk1[:, k, c * P:(c + 1) * P], ctx1[:, k, :], start=k == 0, stop=k == DC - 1)
                last.then_inc(S["kv1_ready"], 1)
            pe.wait_ge(F[0]["y_out"], FT + 1)
            for b in range(NB):
                dst = ps[:, 4 + b // 2, (b % 2) * D:(b % 2 + 1) * D]
                for r in range(2):
                    for k in range(DC):
                        mm(dst[64 * r:64 * r + 64, :], ctx1[:, k, b * KEYS:(b + 1) * KEYS], wv1[:, k, :], start=k == 0, stop=False)
                    last = mm(dst[64 * r:64 * r + 64, :], onesf[:, 0:KEYS], bv1s, start=False, stop=True)
                if b % 2:
                    last.then_inc(S["kv1_ready"], 1)
            pe.wait_ge(S["w1_split"], 1)
            pe.wait_ge(S["kv1_copied"], 4)

            def attention1(n, old, new, following):
                if not new:
                    turn_rows(1, n - 1, xnr_last)
                    logits(1, n - 1)
                    counts(1, n - 1)
                    return
                pe.wait_ge(S["xl1"], 2 * n + 2)
                for c in range(DC):
                    passes(ps[:, S_BANK[0] + c, :], [(wq1h[:, k, c * P:(c + 1) * P], wq1l[:, k, c * P:(c + 1) * P]) for k in range(DC)],
                           [(xth[:, :, k, :], xtl[:, :, k, :]) for k in range(DC)]).then_inc(S["q1_ready"], 1)
                pe.wait_ge(S["q1_evac"], 2 * n + 2)
                pe.wait_ge(S["kb1_ready"], 5 * n + 4)

                def scores(j):
                    if j >= 2:
                        pe.wait_ge(S["score1_shifted"], TB * n + (j - 1))
                    for c in range(DC):
                        q = slice(j * P, (j + 1) * P)
                        last = passes(ps[:, S_BANK[j % 2] + c, :], [(qh[:, c, q], ql[:, c, q])], [(kbh[:, c, :], kbl[:, c, :])])
                    last.then_inc(S["score1_ready"], 1)

                def exps(j):
                    pe.wait_ge(S["exp1_ready"], TB * n + (j + 1))
                    for h in range(2):
                        if j:
                            pe.wait_ge(S["el1"], 2 * TB * n + (2 * j - 1 + h))
                        for i in range(4):
                            at = (4 * h + i) * P
                            last = nc.tensor.transpose(ps[:, 6 + h, i * P:(i + 1) * P], es[:, at:at + P], ident[:])
                        last.then_inc(S["exp1_turned"], 1)

                def values(j):
                    pe.wait_ge(S["el1"], 2 * TB * n + (2 * j + 2))
                    if j == 0:
                        pe.wait_ge(S["kb1_ready"], 5 * n + 5)
                    if j >= 2:
                        pe.wait_ge(S["ctx1_ready"], TB * n + (j - 1))
                    if old and j == 2:
                        pe.wait_ge(S["count1_taken"], n)
                    for a_ in range(PAIRS):
                        last = passes(ps[:, j % 2, a_ * 34:(a_ + 1) * 34], [(eth[:, a_, :], etl[:, a_, :])], [(vbh[:, a_, :], vbl[:, a_, :])])
                    last.then_inc(S["pv1_ready"], 1)
                def turn_context(h):
                    pe.wait_ge(S["ctx1_ready"], TB * n + 2 * (h + 1))
                    for j in range(2):
                        for c in range(DC):
                            at = j * D + c * P
                            last = nc.tensor.transpose(ps[:, S_BANK[0] + h, at:at + P], xn[:, 2 * h + j, c * P:(c + 1) * P], ident[:])
                    last.then_inc(S["ctx1_turned"], 1)

                def output(h):
                    pe.wait_ge(S["cl1"], 2 * n + (h + 1))
                    for j in (2 * h, 2 * h + 1):
                        dst = ps[:, O_BANK[1] + h, (j % 2) * D:(j % 2 + 1) * D]
                        passes(dst, [(xth[:, j, c, :], xtl[:, j, c, :]) for c in range(DC)],
                               [(wo1h[:, c, :], wo1l[:, c, :]) for c in range(DC)], stop=False)
                        mm(dst, rowscale[:], bo1h, start=False, stop=False)
                        last = mm(dst, rowscale[:], bo1l, start=False, stop=True)
                    last.then_inc(S["attn1_ready"], 1)
                scores(0)
                scores(1)
                if old:
                    turn_rows(1, n - 1, xnr)
                    logits(1, n - 1)
                for j in range(TB):
                    exps(j)
                    if j + 2 < TB:
                        scores(j + 2)
                    if j == 2:
                        turn_context(0)
                    if j == 3:
                        output(0)
                    values(j)
                    if old and j == 1:
                        pe.wait_ge(S["ctx1_ready"], TB * n + 1)
                        counts(1, n - 1)
                turn_context(1)
                output(1)
                if following:
                    turn_new(1, n + 1)
            turn_new(1, 0)
            attention1(0, False, True, True)
            with pe.Fori(1, NB - 1) as n:
                attention1(n, True, True, True)
            attention1(NB - 1, True, True, False)
            attention1(NB, True, False, False)
            experts(1)


def kernel(**inputs):
    import numpy as np
    import concourse.bacc as bacc
    from concourse.bass_utils import run_bass_kernel_spmd

    a = {k: np.asarray(v) for k, v in inputs.items()}

    def rows128(m):
        return np.ascontiguousarray(m.reshape(-1, P, *m.shape[1:]).swapaxes(0, 1))

    def expert_weights(firsts, second):
        up = np.concatenate(firsts, axis=2).reshape(E, DC, P, -1).transpose(2, 0, 1, 3).reshape(P, E, -1)
        down = second.reshape(E, -1, P, D).transpose(2, 0, 1, 3).reshape(P, E, -1)
        return np.ascontiguousarray(np.concatenate([up, down], axis=2))

    def columns(*vs):
        return np.ascontiguousarray(np.stack([v.reshape(DC, P).T for v in vs], axis=1))

    ins = {
        "x": a["x"].reshape(NT, P, D),
        "ctxT": rows128(a["ctx_1024"].reshape(NB * KEYS, D).T),
        "gates": np.ascontiguousarray(np.broadcast_to(
            np.stack([a["g_xattn"][0], a["g_ffn"][0], a["g_xattn"][1], a["g_ffn"][1]]), (P, 4))),
        "w_attn0": np.stack([rows128(m) for m in (a["L0_xattn_Wk"].T, a["L0_xattn_Wv"].T, a["L0_xattn_Wq"], a["L0_xattn_Wo"].T)]),
        "b_attn0": columns(a["L0_xattn_bk"], a["L0_xattn_bv"], a["L0_xattn_bq"]),
        "bo0": a["L0_xattn_bo"].reshape(1, D),
        "rt0": rows128(a["L0_ffn_router_w"].T),
        "w_attn1": np.stack([rows128(a[f"L1_xattn_W{n}"].reshape(D, D)) for n in "kvqo"]),
        "b_attn1": columns(a["L1_xattn_bk"].reshape(D), a["L1_xattn_bq"].reshape(D)),
        "bv1": a["L1_xattn_bv"].reshape(1, D),
        "bo1": a["L1_xattn_bo"].reshape(1, D),
        "rt1": rows128(a["L1_ffn_Wg"].T),
        "w_ffn0": expert_weights([a["L0_ffn_w1"]], a["L0_ffn_w2"]),
        "w_ffn1": expert_weights([a["L1_ffn_W1"].transpose(0, 2, 1), a["L1_ffn_W2"].transpose(0, 2, 1)],
                                 a["L1_ffn_W3"].transpose(0, 2, 1)),
    }
    nc = bacc.Bacc("TRN2", target_bir_lowering=False, num_devices=1)
    args = {k: nc.dram_tensor(f"in_{k}", m.shape, mybir.dt.from_np(m.dtype), kind="ExternalInput").ap() for k, m in ins.items()}
    out = nc.dram_tensor("out", (NT, P, D), F32, kind="ExternalOutput").ap()
    build(nc, **args, out=out)
    r = run_bass_kernel_spmd(nc, [{f"in_{k}": m for k, m in ins.items()}], core_ids=[0])
    return r.results[0]["out"].reshape(NB, SEQ, D)
```
